# Optimizing a Trainium2 kernel written in Bass

```python
import numpy as np
import jax
import jax.numpy as jnp

def _softmax(x, axis=-1):
    return jax.nn.softmax(x, axis=axis)

def _gelu(x):
    return jax.nn.gelu(x, approximate=True)

def _silu(x):
    return jax.nn.silu(x)

def _sigmoid(x):
    return jax.nn.sigmoid(x)

def _layernorm(x, axis=-1, eps=1e-05):
    m = jnp.mean(x, axis=axis, keepdims=True)
    v = jnp.var(x, axis=axis, keepdims=True)
    return (x - m) / jnp.sqrt(v + eps)

def _scatter_add(tgt, idx, src, axis=0):
    return tgt.at[idx].add(src)

def _segment_sum(src, seg, n):
    return jax.ops.segment_sum(src, seg, n)
kernel_name = 'mk_adj_resnorm_d4_adj_r2_1fc1b8'

def setup_inputs(seed: int=0):
    np.random.seed(seed)
    _w = jnp.asarray

    def _rec_inputs():
        import jax
        import jax.numpy as jnp
        _gk = jax.random.key(seed)
        x = 7.22e-05 + 1 * jax.random.normal(jax.random.fold_in(_gk, 1), (64, 128, 256), jnp.float32)
        _w = (1.0 + jnp.arange(128, dtype=jnp.float32)) ** (-0.5)
        _w = _w / _w.mean()
        _pij = jnp.clip(0.125 * _w[:, None] * _w[None, :], 0.0, 1.0)
        _a = jax.random.uniform(jax.random.fold_in(_gk, 2), (128, 128)) < _pij
        _a = jnp.logical_or(_a, jnp.eye(128, dtype=bool))
        adj = _a.astype(jnp.int32)
        return (x, adj)
    x, adj = _rec_inputs()

    def _L0_gnn_setup():
        import jax, jax.numpy as jnp
        import numpy as np
        B, N, D = (8, 1024, 256)
        NEG_SLOPE = 0.2
        key = jax.random.key(seed)
        k1, k2, k3, k4, k5 = jax.random.split(key, 5)
        x = jax.random.normal(k1, (B, N, D), dtype=jnp.float32)
        adj = jax.random.randint(k2, (N, N), 0, 2, dtype=jnp.int32)
        adj = jnp.maximum(adj, jnp.eye(N, dtype=jnp.int32))
        W = jax.random.normal(k3, (D, D), dtype=jnp.float32) * (1.0 / np.sqrt(D))
        a_src = jax.random.normal(k4, (D,), dtype=jnp.float32) * (1.0 / np.sqrt(D))
        a_dst = jax.random.normal(k5, (D,), dtype=jnp.float32) * (1.0 / np.sqrt(D))
        return {'x': x, 'adj': adj, 'W': W, 'a_src': a_src, 'a_dst': a_dst}
    _L0_gnn_all = _L0_gnn_setup()
    _L0_gnn_in = {k: v for k, v in _L0_gnn_all.items() if k in ('W', 'a_src', 'a_dst')}
    del _L0_gnn_all

    def _L1_gnn_setup():
        import jax, jax.numpy as jnp
        import numpy as np
        B, N, F, F1 = (512, 75, 256, 128)
        NEG = -1000000000.0
        ALPHA = 0.2
        key = jax.random.key(seed)
        k1, k2, k3, k4 = jax.random.split(key, 4)
        X = jax.random.normal(k1, (B, N, F), dtype=jnp.float32)
        A = jax.random.randint(k2, (N, N), 0, 2, dtype=jnp.int32)
        W = jax.random.normal(k3, (F, F1), dtype=jnp.float32) * (1.0 / np.sqrt(F))
        a = jax.random.normal(k4, (2, F1, 1), dtype=jnp.float32) * (1.0 / np.sqrt(F1))
        return {'X': X, 'A': A, 'W': W, 'a': a}
    _L1_gnn_all = _L1_gnn_setup()
    _L1_gnn_in = {k: v for k, v in _L1_gnn_all.items() if k in ('W', 'a')}
    del _L1_gnn_all

    def _L2_gnn_setup():
        import jax, jax.numpy as jnp
        import numpy as np
        B, K, DIN, DOUT = (32, 64, 256, 256)
        key = jax.random.key(seed)
        k1, k2, k3, k4 = jax.random.split(key, 4)
        x = jax.random.normal(k1, (B, K, DIN), dtype=jnp.float32)
        adj = jax.random.randint(k2, (K, K), 0, 2, dtype=jnp.int32)
        W = jax.random.normal(k3, (DOUT, 2 * DIN), dtype=jnp.float32) * 0.02
        b = jax.random.normal(k4, (DOUT,), dtype=jnp.float32) * 0.02
        return {'x': x, 'adj': adj, 'W': W, 'b': b}
    _L2_gnn_all = _L2_gnn_setup()
    _L2_gnn_in = {k: v for k, v in _L2_gnn_all.items() if k in ('W', 'b')}
    del _L2_gnn_all

    def _L3_gnn_setup():
        import jax, jax.numpy as jnp
        import numpy as np
        LEAKY_ALPHA = 0.01
        NEG_INF = -1000000000.0
        LN_EPS = 1e-05

        def _gat_heads(x, adj, W, a):
            O = W.shape[-1]
            Wh = jnp.einsum('bnf,hfo->bhno', x, W)
            f1 = jnp.einsum('bhno,ho->bhn', Wh, a[:, :O])
            f2 = jnp.einsum('bhno,ho->bhn', Wh, a[:, O:])
            e = f1[:, :, :, None] + f2[:, :, None, :]
            e = jnp.where(e > 0, e, LEAKY_ALPHA * e)
            e = jnp.where(adj[None, None] > 0, e, NEG_INF)
            attn = jax.nn.softmax(e, axis=-1)
            return jnp.einsum('bhnm,bhmo->bhno', attn, Wh)
        key = jax.random.key(seed)
        ks = jax.random.split(key, 10)
        B, N, F_in, F_hid, H, F_out, D_ff = (8, 1024, 256, 256, 4, 256, 256)
        s = 0.05
        return {'enc_inputs': jax.random.normal(ks[0], (B, N, F_in), jnp.float32), 'adj': jax.random.randint(ks[1], (N, N), 0, 2, jnp.int32), 'W_heads': jax.random.normal(ks[2], (H, F_in, F_hid), jnp.float32) * s, 'a_heads': jax.random.normal(ks[3], (H, 2 * F_hid), jnp.float32) * s, 'W_out': jax.random.normal(ks[4], (H * F_hid, F_out), jnp.float32) * s, 'a_out': jax.random.normal(ks[5], (2 * F_out,), jnp.float32) * s, 'w1': jax.random.normal(ks[6], (F_out, D_ff), jnp.float32) * s, 'b1': jnp.zeros((D_ff,), jnp.float32), 'w2': jax.random.normal(ks[7], (D_ff, F_out), jnp.float32) * s, 'b2': jnp.zeros((F_out,), jnp.float32), 'ln_gamma': jnp.ones((F_out,), jnp.float32), 'ln_beta': jnp.zeros((F_out,), jnp.float32)}
    _L3_gnn_all = _L3_gnn_setup()
    _L3_gnn_in = {k: v for k, v in _L3_gnn_all.items() if k in ('W_heads', 'a_heads', 'W_out', 'a_out', 'w1', 'b1', 'w2', 'b2', 'ln_gamma', 'ln_beta')}
    del _L3_gnn_all
    return {'x': x, 'adj': adj, 'L0_gnn_W': _L0_gnn_in['W'], 'L0_gnn_a_src': _L0_gnn_in['a_src'], 'L0_gnn_a_dst': _L0_gnn_in['a_dst'], 'L1_gnn_W': _L1_gnn_in['W'], 'L1_gnn_a': _L1_gnn_in['a'], 'L2_gnn_W': _L2_gnn_in['W'], 'L2_gnn_b': _L2_gnn_in['b'], 'L3_gnn_W_heads': _L3_gnn_in['W_heads'], 'L3_gnn_a_heads': _L3_gnn_in['a_heads'], 'L3_gnn_W_out': _L3_gnn_in['W_out'], 'L3_gnn_a_out': _L3_gnn_in['a_out'], 'L3_gnn_w1': _L3_gnn_in['w1'], 'L3_gnn_b1': _L3_gnn_in['b1'], 'L3_gnn_w2': _L3_gnn_in['w2'], 'L3_gnn_b2': _L3_gnn_in['b2'], 'L3_gnn_ln_gamma': _L3_gnn_in['ln_gamma'], 'L3_gnn_ln_beta': _L3_gnn_in['ln_beta']}

def reference(x, adj, L0_gnn_W, L0_gnn_a_src, L0_gnn_a_dst, L1_gnn_W, L1_gnn_a, L2_gnn_W, L2_gnn_b, L3_gnn_W_heads, L3_gnn_a_heads, L3_gnn_W_out, L3_gnn_a_out, L3_gnn_w1, L3_gnn_b1, L3_gnn_w2, L3_gnn_b2, L3_gnn_ln_gamma, L3_gnn_ln_beta):
    import jax
    import jax.numpy as jnp

    def _L0_gnn_ref(x, adj, W, a_src, a_dst):
        import jax, jax.numpy as jnp
        import numpy as np
        B, N, D = (8, 1024, 256)
        NEG_SLOPE = 0.2
        Wh = jnp.einsum('bnd,de->bne', x, W)
        e_src = jnp.einsum('bnd,d->bn', Wh, a_src)
        e_dst = jnp.einsum('bnd,d->bn', Wh, a_dst)
        logits = e_src[:, :, None] + e_dst[:, None, :]
        logits = jnp.where(logits >= 0, logits, NEG_SLOPE * logits)
        mask = (adj == 0)[None, :, :]
        logits = jnp.where(mask, -jnp.inf, logits)
        attn = jax.nn.softmax(logits, axis=-1)
        attn = jnp.nan_to_num(attn, nan=0.0)
        out = jnp.einsum('bnm,bmd->bnd', attn, Wh)
        return out

    def _L1_gnn_ref(X, A, W, a):
        import jax, jax.numpy as jnp
        import numpy as np
        B, N, F, F1 = (512, 75, 256, 128)
        NEG = -1000000000.0
        ALPHA = 0.2
        h = jnp.einsum('bnf,fo->bno', X, W)
        att_self = jnp.einsum('bno,od->bnd', h, a[0])
        att_neigh = jnp.einsum('bno,od->bnd', h, a[1])
        e = att_self + jnp.swapaxes(att_neigh, 1, 2)
        e = jax.nn.leaky_relu(e, ALPHA)
        adj = A.astype(h.dtype)
        e = e + NEG * (1.0 - adj)[None, :, :]
        alpha = jax.nn.softmax(e, axis=-1)
        out = jnp.einsum('bij,bjo->bio', alpha, h)
        return jnp.concatenate([out, h], axis=-1)

    def _L2_gnn_ref(x, adj, W, b):
        import jax, jax.numpy as jnp
        import numpy as np
        B, K, DIN, DOUT = (32, 64, 256, 256)
        Din = x.shape[-1]
        Wi, Wj = (W[:, :Din], W[:, Din:])
        mi = jnp.einsum('bkd,od->bko', x, Wi)
        mj = jnp.einsum('bkd,od->bko', x, Wj)
        a = adj.astype(x.dtype)
        deg = a.sum(axis=1)
        out = deg[None, :, None] * (mi + b) + jnp.einsum('ij,bjo->bio', a, mj)
        return out

    def _L3_gnn_ref(enc_inputs, adj, W_heads, a_heads, W_out, a_out, w1, b1, w2, b2, ln_gamma, ln_beta):
        import jax, jax.numpy as jnp
        import numpy as np
        LEAKY_ALPHA = 0.01
        NEG_INF = -1000000000.0
        LN_EPS = 1e-05

        def _gat_heads(x, adj, W, a):
            O = W.shape[-1]
            Wh = jnp.einsum('bnf,hfo->bhno', x, W)
            f1 = jnp.einsum('bhno,ho->bhn', Wh, a[:, :O])
            f2 = jnp.einsum('bhno,ho->bhn', Wh, a[:, O:])
            e = f1[:, :, :, None] + f2[:, :, None, :]
            e = jnp.where(e > 0, e, LEAKY_ALPHA * e)
            e = jnp.where(adj[None, None] > 0, e, NEG_INF)
            attn = jax.nn.softmax(e, axis=-1)
            return jnp.einsum('bhnm,bhmo->bhno', attn, Wh)
        B, N, _ = enc_inputs.shape
        h = jax.nn.elu(_gat_heads(enc_inputs, adj, W_heads, a_heads))
        h = jnp.transpose(h, (0, 2, 1, 3)).reshape(B, N, -1)
        out = _gat_heads(h, adj, W_out[None], a_out[None])[:, 0]
        out = jax.nn.elu(out)
        ffn = jnp.maximum(out @ w1 + b1, 0.0) @ w2 + b2
        y = ffn + out
        mu = jnp.mean(y, axis=-1, keepdims=True)
        var = jnp.var(y, axis=-1, keepdims=True)
        return (y - mu) / jnp.sqrt(var + LN_EPS) * ln_gamma + ln_beta
    x = _layernorm(x + _L0_gnn_ref(x, adj, L0_gnn_W, L0_gnn_a_src, L0_gnn_a_dst), axis=-1)
    x = _layernorm(x + _L1_gnn_ref(x, adj, L1_gnn_W, L1_gnn_a), axis=-1)
    x = _layernorm(x + _L2_gnn_ref(x, adj, L2_gnn_W, L2_gnn_b), axis=-1)
    x = _layernorm(x + _L3_gnn_ref(x, adj, L3_gnn_W_heads, L3_gnn_a_heads, L3_gnn_W_out, L3_gnn_a_out, L3_gnn_w1, L3_gnn_b1, L3_gnn_w2, L3_gnn_b2, L3_gnn_ln_gamma, L3_gnn_ln_beta), axis=-1)
    return x

_drawn_inputs = setup_inputs


def setup_inputs(seed=0):
    import zlib

    import numpy as np

    out = dict(_drawn_inputs(seed))
    spreads = {'L3_gnn_b1': (0.0, 0.1),
     'L3_gnn_b2': (0.0, 0.1),
     'L3_gnn_ln_gamma': (1.0, 0.2),
     'L3_gnn_ln_beta': (0.0, 0.1)}
    factors = {}
    for name, (base, spread) in spreads.items():
        noise = np.random.default_rng([zlib.crc32(name.encode()), seed]).standard_normal(out[name].shape)
        drawn = base * np.exp(spread * noise) if base else spread * noise
        out[name] = jnp.asarray(drawn.astype(out[name].dtype))
    for name, factor in factors.items():
        out[name] = (out[name] * factor).astype(out[name].dtype)
    return out
```

```python
import concourse.bass as bass
import concourse.mybir as mybir
import numpy as np
from contextlib import ExitStack

B, N, D = 64, 128, 256
G = 2
UNITS = B // G
P = 128
DC = D // P
F1 = 128
H = 4
HC = H * DC
SLOPE_L0, SLOPE_L1, SLOPE_L3 = 0.2, 0.2, 0.01
FAR = -2.0 ** 100
EPS = 1e-5

F32 = mybir.dt.float32
F32R = mybir.dt.float32r
I32 = mybir.dt.int32
ALU = mybir.AluOpType
ACT = mybir.ActivationFunctionType
AX = mybir.AxisListType


W0_COLUMNS = 2 * DC
W1_COLUMNS = W0_COLUMNS + 2 * DC
WH_COLUMNS = W1_COLUMNS + 2 * H * DC
WO_COLUMNS = WH_COLUMNS + 2 * HC


class Stage:

    def __init__(self, n, again):
        self.n = n
        self.before = n - 1
        self.again = again


class Turn:

    def __init__(self, t, looped=False):
        self.t = t
        self.stages = []
        for lag in range(4):
            if looped:
                self.stages.append(Stage(t + (1 - lag), True))
            elif 0 <= t - lag < UNITS:
                self.stages.append(Stage(t - lag + 1, t - lag > 0))
            else:
                self.stages.append(None)
        self.a, self.b, self.c, self.d = self.stages
        self.loads = looped or t + 1 < UNITS


FIRST_LOOPED, LAST_LOOPED = 4, UNITS - 2


def run_turns(eng, body, between=None):
    for t in range(FIRST_LOOPED):
        body(Turn(t))
        if between:
            between(t)
    with eng.Fori(FIRST_LOOPED, LAST_LOOPED + 1) as t:
        body(Turn(t, looped=True))
    for t in range(LAST_LOOPED + 1, UNITS + 3):
        body(Turn(t))


def build(nc, x, adj, adj_t, w0, a0_src, a0_dst, w1, a1, w2_t, b2, wh, ah, wo, ao,
          ff1, fb1_t, ff2, fb2, gamma, beta, out):
    ctx = ExitStack()
    with ctx:
        def sb(name, shape, dt=F32):
            return ctx.enter_context(nc.sbuf_tensor(name, shape, dt))

        def bank(name):
            return ctx.enter_context(nc.psum_tensor(name, [P, 512], F32))

        def sem(name):
            return ctx.enter_context(nc.semaphore(name))

        ident = sb("ident", [P, P])
        ident_r = sb("ident_r", [P, P], F32R)
        adj_i = sb("adj_i", [P, P], I32)
        adj_ti = sb("adj_ti", [P, P], I32)
        mask = sb("mask", [P, P], F32R)
        nonzero = sb("nonzero", [P, P])
        has_neighbour = sb("has_neighbour", [P, 1])
        degree = sb("degree", [P, 1])
        adj_deg = sb("adj_deg", [P, 2, P], F32R)
        deg_b = sb("deg_b", [P, D])
        eps_c = sb("eps_c", [P, G])
        half_c = sb("half_c", [P, G])
        b2_bc = sb("b2_bc", [P, D])
        fb2_bc = sb("fb2_bc", [P, D])
        gamma_bc = sb("gamma_bc", [P, D])
        beta_bc = sb("beta_bc", [P, D])
        fb1_c = sb("fb1_c", [P, DC])
        a0_bc = sb("a0_bc", [P, 2, D])
        a1_bc = sb("a1_bc", [P, 2, F1])
        ah_bc = sb("ah_bc", [P, H, 2, D])
        ao_bc = sb("ao_bc", [P, 2, D])
        junk = sb("junk", [P, D])
        w0_s = sb("w0_s", [P, DC, D + 2])
        w0_h = sb("w0_h", [P, DC, D + 2], F32R)
        w0_l = sb("w0_l", [P, DC, D + 2], F32R)
        w1_s = sb("w1_s", [P, DC, F1 + 2])
        w1_h = sb("w1_h", [P, DC, F1 + 2], F32R)
        w1_l = sb("w1_l", [P, DC, F1 + 2], F32R)
        w2_s = sb("w2_s", [P, 2, DC, D])
        wh_s = sb("wh_s", [P, DC, H * D])
        wh_h = sb("wh_h", [P, DC, H * D], F32R)
        wh_l = sb("wh_l", [P, DC, H * D], F32R)
        wa_s = sb("wa_s", [P, DC, 2 * H])
        wa_h = sb("wa_h", [P, DC, 2 * H], F32R)
        wa_l = sb("wa_l", [P, DC, 2 * H], F32R)
        wo_s = sb("wo_s", [P, HC, D + 2])
        ff1_s = sb("ff1_s", [P, DC, D])
        ff2_s = sb("ff2_s", [P, DC, D])

        PS = [[bank(f"{s}{k}") for k in range(2)] for s in "abcd"]
        (bank_a0, bank_a1), (bank_b0, bank_b1), (bank_c0, bank_c1), (bank_d0, bank_d1) = PS

        class Attention:

            def __init__(self, name, slope, scores, probs, proj, width):
                self.slope = slope
                self.scores, self.probs = scores, probs
                self.proj = proj
                self.s = proj[:, :, width:width + 1]
                self.d = proj[:, :, width + 1:width + 2]
                self.top = sb(f"{name}_top", [P, G])
                self.neg = sb(f"{name}_neg", [P, G])
                self.neg_max = sb(f"{name}_neg_max", [P, G])
                self.bias = sb(f"{name}_bias", [P, 2, G])
                self.e1 = sb(f"{name}_e1", [P, G, P])
                self.e2 = sb(f"{name}_e2", [P, G, P])
                self.p = sb(f"{name}_p", [P, G, P])
                self.sum = sb(f"{name}_sum", [P, G])
                self.rsum = sb(f"{name}_rsum", [P, G])
                self.p_t = sb(f"{name}_p_t", [P, G, P])
                self.scored = sem(f"{name}_scored")
                self.maxing = sem(f"{name}_maxing")
                self.biased = sem(f"{name}_biased")
                self.expd = sem(f"{name}_expd")
                self.weighed = sem(f"{name}_weighed")
                self.inverted = sem(f"{name}_inverted")
                self.turned = sem(f"{name}_turned")
                self.kept = sem(f"{name}_kept")

        class Norm:

            def __init__(self, name):
                self.y = sb(f"{name}_y", [P, G, D])
                self.stats = sb(f"{name}_stats", [P, G, 6])
                self.moments = sb(f"{name}_moments", [P, G, 2])
                self.var_eps = sb(f"{name}_var_eps", [P, G])
                self.rstd = sb(f"{name}_rstd", [P, G])
                self.summed = sem(f"{name}_summed")
                self.averaged = sem(f"{name}_averaged")
                self.scaled = sem(f"{name}_scaled")
                self.done = sem(f"{name}_done")

        x0 = sb("x0", [P, G, D])
        xt0_h = sb("xt0_h", [P, DC, G, P], F32R)
        xt0_l = sb("xt0_l", [P, DC, G, P], F32R)
        proj0 = sb("proj0", [P, G, D + 2])
        x1 = sb("x1", [P, G, D])
        att0 = Attention("att0", SLOPE_L0, bank_a0, bank_a1, proj0, D)
        gated0 = sem("gated0")
        norm0 = Norm("norm0")
        xt1_h = sb("xt1_h", [P, DC, G, P], F32R)
        xt1_l = sb("xt1_l", [P, DC, G, P], F32R)
        proj1 = sb("proj1", [P, G, F1 + 2])
        x2 = sb("x2", [P, G, D])
        x2_h = sb("x2_h", [P, G, D], F32R)
        x2_l = sb("x2_l", [P, G, D], F32R)
        x2_b = sb("x2_b", [P, G, D])
        conv_t = sb("conv_t", [P, G, DC, 2, P])
        att1 = Attention("att1", SLOPE_L1, bank_b0, bank_b1, proj1, F1)
        norm1, norm2 = Norm("norm1"), Norm("norm2")
        x3 = sb("x3", [P, G, D])
        xt3_h = sb("xt3_h", [P, DC, G, P], F32R)
        xt3_l = sb("xt3_l", [P, DC, G, P], F32R)
        proj3 = sb("proj3", [P, G, H * D])
        sd3 = sb("sd3", [P, G, 2 * H])
        top3 = sb("top3", [P, G, H])
        neg3 = sb("neg3", [P, G, H])
        neg_max3 = sb("neg_max3", [P, G, H])
        bias3 = sb("bias3", [P, G, 2, H])
        e13 = sb("e13", [P, G, H, P])
        e23 = sb("e23", [P, G, H, P])
        p3 = sb("p3", [P, G, H, P])
        sum3 = sb("sum3", [P, G, H])
        rsum3 = sb("rsum3", [P, G, H])
        p3_t = sb("p3_t", [P, G, H, P])
        elu3 = sb("elu3", [P, 2, 512])
        h_t = sb("h_t", [P, H, DC, G, P])
        proj4 = sb("proj4", [P, G, D + 2])
        att4 = Attention("att4", SLOPE_L3, bank_d0, bank_d1, proj4, D)
        elu4 = sb("elu4", [P, 512])
        o_t = sb("o_t", [P, DC, G * P])
        relu_t = sb("relu_t", [P, DC, G * P])
        x3_b = sb("x3_b", [P, 2 * G, D])
        norm3, norm4 = Norm("norm3"), Norm("norm4")
        n3 = sb("n3", [P, G, D])
        n3_g = sb("n3_g", [P, G, D])
        result = sb("result", [P, G, D])

        made = sem("made")
        ident_made = sem("ident_made")
        adj_in, vec_in = sem("adj_in"), sem("vec_in")
        w0_in, w1_in, w2_in = sem("w0_in"), sem("w1_in"), sem("w2_in")
        wh_in, wo_in, ff_in = sem("wh_in"), sem("wo_in"), sem("ff_in")
        adj_made = sem("adj_made")
        attended = sem("attended")
        w0_hi, w1_hi, wh_hi = sem("w0_hi"), sem("w1_hi"), sem("wh_hi")
        w0_lo, w1_lo, wh_lo = sem("w0_lo"), sem("w1_lo"), sem("wh_lo")
        x0_in = sem("x0_in")
        stored = sem("stored")
        xt0, xt1, xt3 = sem("xt0"), sem("xt1"), sem("xt3")
        hi0, hi1, hi3 = sem("hi0"), sem("hi1"), sem("hi3")
        lo0, lo1, lo3 = sem("lo0"), sem("lo1"), sem("lo3")
        projected0 = [sem(f"projected0_{b}") for b in range(G)]
        projected1 = sem("projected1")
        proj0_kept, proj1_kept = sem("proj0_kept"), sem("proj1_kept")
        mixed0, mixed1 = sem("mixed0"), sem("mixed1")
        x2_hi, x2_lo, x2_biased = sem("x2_hi"), sem("x2_lo"), sem("x2_biased")
        conv = [sem(f"conv_{b}") for b in range(G)]
        conv_kept = [sem(f"conv_kept_{b}") for b in range(G)]
        conv_out = sem("conv_out")
        scored_c, sd_kept = sem("scored_c"), sem("sd_kept")
        head_proj = [sem(f"head_proj_{k}") for k in range(4)]
        head_proj_kept = [sem(f"head_proj_kept_{k}") for k in range(4)]
        z3 = [sem(f"z3_{b}") for b in range(G)]
        maxing3 = [sem(f"maxing3_{b}") for b in range(G)]
        biased3 = [sem(f"biased3_{b}") for b in range(G)]
        expd3 = [sem(f"expd3_{b}") for b in range(G)]
        weighed3 = [sem(f"weighed3_{b}") for b in range(G)]
        inverted3 = [sem(f"inverted3_{b}") for b in range(G)]
        normal3 = [sem(f"normal3_{b}") for b in range(G)]
        turned3 = [sem(f"turned3_{b}") for b in range(G)]
        kept3 = [sem(f"kept3_{b}") for b in range(G)]
        mixed3 = [sem(f"mixed3_{h}") for h in range(H)]
        elu_exp3 = [sem(f"elu_exp3_{h}") for h in range(H)]
        elu_low3 = [sem(f"elu_low3_{h}") for h in range(H)]
        h_ready = [sem(f"h_ready_{h}") for h in range(H)]
        projected4 = [sem(f"projected4_{b}") for b in range(G)]
        proj4_kept = sem("proj4_kept")
        normal4 = sem("normal4")
        mixed4, elu_exp4, elu_low4, o_ready = sem("mixed4"), sem("elu_exp4"), sem("elu_low4"), sem("o_ready")
        ff1_out, relu_ready, ff2_out = sem("ff1_out"), sem("relu_ready"), sem("ff2_out")
        scaled3, x3_biased = sem("scaled3"), sem("x3_biased")
        block = ctx.enter_context(nc.Block())

        @block.sync
        def _(sp):
            def unit(src, n):
                return src[bass.ds(n * G, G), :, :].rearrange("b n d -> n b d")

            sp.dma_start(x0[:, :, :], unit(x, 0)).then_inc(x0_in, 16)
            sp.dma_start(w0_s[:, :, 0:D], w0.rearrange("(c p) f -> p c f", p=P)).then_inc(w0_in, 16)
            sp.dma_start(adj_i[:, :], adj[:, :]).then_inc(adj_in, 16)
            sp.dma_start(adj_ti[:, :], adj_t[:, :]).then_inc(adj_in, 16)
            sp.dma_start(w1_s[:, :, 0:F1], w1.rearrange("(c p) f -> p c f", p=P)).then_inc(w1_in, 16)
            sp.dma_start(w2_s[:, :, :, :], w2_t.rearrange("(k c p) f -> p k c f", k=2, p=P)).then_inc(w2_in, 16)
            for h in range(H):
                sp.dma_start(wh_s[:, :, h * D:(h + 1) * D],
                             wh[h, :, :].rearrange("(c p) f -> p c f", p=P)).then_inc(wh_in, 16)
            sp.dma_start(wo_s[:, :, 0:D], wo.rearrange("(c p) f -> p c f", p=P)).then_inc(wo_in, 16)
            sp.dma_start(ff1_s[:, :, :], ff1.rearrange("(c p) f -> p c f", p=P)).then_inc(ff_in, 16)
            sp.dma_start(ff2_s[:, :, :], ff2.rearrange("(c p) f -> p c f", p=P)).then_inc(ff_in, 16)

            def turn(u):
                if u.loads:
                    sp.wait_ge(norm0.summed, u.a.n)
                    sp.dma_start(x0[:, :, :], unit(x, u.a.n)).then_inc(x0_in, 16)
                if u.d:
                    sp.wait_ge(norm4.done, u.d.n)
                    sp.dma_start(unit(out, u.d.before), result[:, :, :]).then_inc(stored, 16)

            run_turns(sp, turn)
            sp.wait_ge(stored, 16 * UNITS)

        @block.gpsimd
        def _(pool):
            def over_rows(v):
                return v.rearrange("(a n) -> a n", a=1).to_broadcast([P, v.shape[0]])

            pool.memset(ident[:, :], 0.0).then_inc(made, 1)
            pool.memset(eps_c[:, :], EPS).then_inc(made, 1)
            pool.memset(half_c[:, :], -0.5).then_inc(made, 1)
            pool.wait_ge(made, 3)
            pool.affine_select(out=ident[:, :], in_=ident[:, :], compare_op=ALU.not_equal, fill=1.0, base=0,
                               pattern=[[-1, P]], channel_multiplier=1).then_inc(made, 1)
            pool.wait_ge(made, 4)

            def rstd(norm, n):
                pool.wait_ge(norm.averaged, n * 2)
                pool.tensor_tensor(norm.var_eps[:, :], norm.moments[:, :, 1], eps_c[:, :], ALU.add)\
                    .then_inc(norm.scaled, 1)
                pool.wait_ge(norm.scaled, n * 2 - 1)
                pool.tensor_tensor(norm.rstd[:, :], norm.var_eps[:, :], half_c[:, :], ALU.pow)\
                    .then_inc(norm.scaled, 1)

            def normalise_heads(s, b):
                pool.wait_ge(inverted3[b], s.n)
                pool.tensor_tensor(p3[:, b, :, :], p3[:, b, :, :],
                                   rsum3[:, b, :].unsqueeze(2).to_broadcast([P, H, P]), ALU.mult)\
                    .then_inc(normal3[b], 1)

            def turn(u):
                if u.c:
                    normalise_heads(u.c, 0)
                    pool.tensor_tensor(x3_b[:, bass.ds(u.t % 2 * G, G), :], x3[:, :, :],
                                       beta_bc[:, :].unsqueeze(1).to_broadcast([P, G, D]), ALU.add)\
                        .then_inc(x3_biased, 1)
                if u.d:
                    pool.wait_ge(att4.inverted, u.d.n)
                    pool.tensor_tensor(att4.p[:, :, :], att4.p[:, :, :],
                                       att4.rsum[:, :].unsqueeze(2).to_broadcast([P, G, P]), ALU.mult)\
                        .then_inc(normal4, 1)
                if u.a:
                    rstd(norm0, u.a.n)
                if u.b:
                    rstd(norm1, u.b.n)
                if u.c:
                    normalise_heads(u.c, 1)
                if u.b:
                    pool.wait_ge(x2_hi, u.b.n)
                    pool.tensor_tensor(x2_l[:, :, :], x2[:, :, :], x2_h[:, :, :].bitcast(F32), ALU.subtract)\
                        .then_inc(x2_lo, 1)
                    pool.tensor_tensor(x2_b[:, :, :], x2[:, :, :],
                                       deg_b[:, :].unsqueeze(1).to_broadcast([P, G, D]), ALU.add)\
                        .then_inc(x2_biased, 1)
                if u.d:
                    rstd(norm3, u.d.n)
                    pool.wait_ge(norm3.done, u.d.n)
                    pool.tensor_tensor(n3_g[:, :, :], n3[:, :, :],
                                       gamma_bc[:, :].unsqueeze(1).to_broadcast([P, G, D]), ALU.mult)\
                        .then_inc(scaled3, 1)
                if u.b:
                    rstd(norm2, u.b.n)
                if u.d:
                    rstd(norm4, u.d.n)

            for dst, src in ((a0_bc[:, 0, :], a0_src), (a0_bc[:, 1, :], a0_dst)):
                pool.dma_start(dst, over_rows(src)).then_inc(vec_in, 16)
            for k in range(2):
                pool.dma_start(a1_bc[:, k, :], over_rows(a1[k, :])).then_inc(vec_in, 16)
            pool.dma_start(b2_bc[:, :], over_rows(b2)).then_inc(vec_in, 16)
            for h in range(H):
                pool.dma_start(ah_bc[:, h, :, :].rearrange("p k f -> p (k f)"), over_rows(ah[h, :]))\
                    .then_inc(vec_in, 16)
            pool.dma_start(ao_bc[:, :, :].rearrange("p k f -> p (k f)"), over_rows(ao)).then_inc(vec_in, 16)
            for dst, src in ((fb2_bc, fb2), (gamma_bc, gamma), (beta_bc, beta)):
                pool.dma_start(dst[:, :], over_rows(src)).then_inc(vec_in, 16)
            pool.dma_start(fb1_c[:, :], fb1_t[:, :]).then_inc(vec_in, 16)
            pool.wait_ge(adj_made, 7)
            pool.wait_ge(vec_in, 16 * 14)
            run_turns(pool, turn)

        @block.tensor
        def _(pe):
            def transpose_x(src, dst):
                for c in range(DC):
                    for b in range(G):
                        k = c * G + b
                        last = nc.tensor.transpose(dst[:, k * P:(k + 1) * P], src[:, b, c * P:(c + 1) * P],
                                                   ident[:, :])
                return last

            def split_product(dst, xt_h, xt_l, b, w_h, w_l, cols):
                pairs = [(c, x_part, w_part) for x_part, w_part in ((xt_l, w_h), (xt_h, w_l), (xt_h, w_h))
                         for c in range(DC)]
                for k, (c, x_part, w_part) in enumerate(pairs):
                    last = nc.tensor.matmul(dst, x_part[:, c, b, :], w_part[:, c, cols],
                                            start=(k == 0), stop=(k == len(pairs) - 1))
                return last

            def scores(att, n):
                nc.tensor.matmul(att.scores[:, 0:G * P], ident_r[:, :],
                                 mask[:, :].unsqueeze(1).to_broadcast([P, G, P]), start=True, stop=False)
                for b in range(G):
                    last = nc.tensor.matmul(att.scores[:, b * P:(b + 1) * P],
                                            att.d[:, b, :].to_broadcast([P, P]), ident[:, :],
                                            is_transpose=True, start=False, stop=(b == G - 1))
                last.then_inc(att.scored, 1)

            def turn_weights(att, n):
                for b in range(G):
                    last = nc.tensor.transpose(att.probs[:, b * P:(b + 1) * P], att.p[:, b, :], ident[:, :])
                last.then_inc(att.turned, 1)

            def a_transpose(s):
                pe.wait_ge(x0_in, s.n * 16)
                if s.again:
                    pe.wait_ge(norm0.summed, s.before)
                transpose_x(x0, bank_a0).then_inc(xt0, 1)

            def a_project(s):
                pe.wait_ge(lo0, s.n)
                for b, dst in enumerate((bank_a0, bank_a1)):
                    split_product(dst[:, 0:D + 2], xt0_h, xt0_l, b, w0_h, w0_l, slice(0, D + 2))\
                        .then_inc(projected0[b], 1)

            def a_scores(s):
                pe.wait_ge(proj0_kept, s.n)
                scores(att0, s.n)

            def a_turn(s):
                pe.wait_ge(att0.weighed, s.n)
                turn_weights(att0, s.n)

            def a_mix(s):
                pe.wait_ge(att0.kept, s.n)
                for b in range(G):
                    last = nc.tensor.matmul(bank_a0[:, b * D:(b + 1) * D], att0.p_t[:, b, :],
                                            proj0[:, b, 0:D], start=True, stop=True)
                last.then_inc(mixed0, 1)

            def b_transpose(s):
                pe.wait_ge(norm0.done, s.n)
                if s.again:
                    pe.wait_ge(conv_kept[1], s.before)
                transpose_x(x1, bank_b0).then_inc(xt1, 1)

            def b_project(s):
                pe.wait_ge(lo1, s.n)
                if s.again:
                    pe.wait_ge(norm2.summed, s.before)
                for b in range(G):
                    last = split_product(bank_b1[:, b * (F1 + 2):(b + 1) * (F1 + 2)], xt1_h, xt1_l, b,
                                         w1_h, w1_l, slice(0, F1 + 2))
                last.then_inc(projected1, 1)

            def b_scores(s):
                pe.wait_ge(proj1_kept, s.n)
                scores(att1, s.n)

            def b_turn(s):
                pe.wait_ge(att1.weighed, s.n)
                turn_weights(att1, s.n)

            def b_mix(s):
                pe.wait_ge(att1.kept, s.n)
                for b in range(G):
                    last = nc.tensor.matmul(bank_b0[:, b * F1:(b + 1) * F1], att1.p_t[:, b, :],
                                            proj1[:, b, 0:F1], start=True, stop=True)
                last.then_inc(mixed1, 1)

            def b_convolve(s):
                pe.wait_ge(x2_lo, s.n)
                for b, dst in enumerate((bank_b1, bank_b0)):
                    for c in range(DC):
                        cols = slice(c * P, (c + 1) * P)
                        for k, part in enumerate((x2_l, x2_h)):
                            last = nc.tensor.matmul(dst[:, c * 2 * P:(c + 1) * 2 * P], part[:, b, cols],
                                                    adj_deg[:, :, :], start=(k == 0), stop=(k == 1))
                    last.then_inc(conv[b], 1)

            def b_conv_project(s):
                pe.wait_ge(conv_kept[0], s.n)
                for b in range(G):
                    if b == 1:
                        pe.wait_ge(conv_kept[1], s.n)
                    for k, (c, which) in enumerate((c, which) for c in range(DC) for which in range(2)):
                        last = nc.tensor.matmul(bank_b1[:, b * D:(b + 1) * D], conv_t[:, b, c, which, :],
                                                w2_s[:, 1 - which, c, :], start=(k == 0), stop=(k == 2 * DC - 1))
                last.then_inc(conv_out, 1)

            def c_transpose(s):
                pe.wait_ge(norm2.done, s.n)
                if s.again:
                    pe.wait_ge(h_ready[2], s.before)
                transpose_x(x3, bank_c0).then_inc(xt3, 1)

            def c_sd(s):
                pe.wait_ge(lo3, s.n)
                if s.again:
                    pe.wait_ge(h_ready[3], s.before)
                for b in range(G):
                    last = split_product(bank_c1[:, b * 2 * H:(b + 1) * 2 * H], xt3_h, xt3_l, b, wa_h, wa_l,
                                         slice(0, 2 * H))
                last.then_inc(scored_c, 1)

            def c_scores(s, b):
                if b == 0:
                    pe.wait_ge(sd_kept, s.n)
                else:
                    pe.wait_ge(expd3[0], s.n)
                nc.tensor.matmul(bank_c0[:, :], ident_r[:, :], mask[:, :].unsqueeze(1).to_broadcast([P, H, P]),
                                 start=True, stop=False)
                for h in range(H):
                    last = nc.tensor.matmul(bank_c0[:, h * P:(h + 1) * P],
                                            sd3[:, b, H + h:H + h + 1].to_broadcast([P, P]), ident[:, :],
                                            is_transpose=True, start=False, stop=(h == H - 1))
                last.then_inc(z3[b], 1)

            def c_project(s, k):
                if k:
                    pe.wait_ge(head_proj_kept[k - 1], s.n)
                half = slice((k % 2) * 512, (k % 2 + 1) * 512)
                split_product(bank_c1[:, :], xt3_h, xt3_l, k // 2, wh_h, wh_l, half).then_inc(head_proj[k], 1)

            def c_turn(s, b):
                pe.wait_ge(normal3[b], s.n)
                if b == 0:
                    pe.wait_ge(expd3[1], s.n)
                else:
                    pe.wait_ge(head_proj_kept[3], s.n)
                for h in range(H):
                    last = nc.tensor.transpose((bank_c0, bank_c1)[b][:, h * P:(h + 1) * P], p3[:, b, h, :],
                                               ident[:, :])
                last.then_inc(turned3[b], 1)

            def c_mix(s, h):
                if h < 2:
                    pe.wait_ge(kept3[1], s.n)
                else:
                    pe.wait_ge(h_ready[h - 2], s.n)
                dst = (bank_c0, bank_c1)[h % 2]
                for c in range(DC):
                    for b in range(G):
                        k = c * G + b
                        last = nc.tensor.matmul(dst[:, k * P:(k + 1) * P],
                                                proj3[:, b, h * D + c * P:h * D + (c + 1) * P],
                                                p3_t[:, b, h, :], start=True, stop=True)
                last.then_inc(mixed3[h], 1)

            def d_project(s, b):
                if b == 0:
                    pe.wait_ge(h_ready[3], s.n)
                    if s.again:
                        pe.wait_ge(norm3.summed, s.before)
                for k in range(HC):
                    last = nc.tensor.matmul((bank_d0, bank_d1)[b][:, 0:D + 2], h_t[:, k // DC, k % DC, b, :],
                                            wo_s[:, k, :], start=(k == 0), stop=(k == HC - 1))
                last.then_inc(projected4[b], 1)

            def d_scores(s):
                pe.wait_ge(proj4_kept, s.n)
                scores(att4, s.n)

            def d_turn(s):
                pe.wait_ge(normal4, s.n)
                turn_weights(att4, s.n)

            def d_mix(s):
                pe.wait_ge(att4.kept, s.n)
                for c in range(DC):
                    for b in range(G):
                        k = c * G + b
                        last = nc.tensor.matmul(bank_d0[:, k * P:(k + 1) * P], proj4[:, b, c * P:(c + 1) * P],
                                                att4.p_t[:, b, :], start=True, stop=True)
                last.then_inc(mixed4, 1)

            def d_ff1(s):
                pe.wait_ge(o_ready, s.n)
                for m in range(DC):
                    for c in range(DC):
                        last = nc.tensor.matmul(bank_d1[:, m * G * P:(m + 1) * G * P],
                                                ff1_s[:, c, m * P:(m + 1) * P], o_t[:, c, :],
                                                start=(c == 0), stop=(c == DC - 1))
                last.then_inc(ff1_out, 1)

            def d_ff2(s):
                pe.wait_ge(relu_ready, s.n)
                for b in range(G):
                    rows = slice(b * P, (b + 1) * P)
                    for c in range(DC):
                        nc.tensor.matmul(bank_d0[:, b * D:(b + 1) * D], relu_t[:, c, rows], ff2_s[:, c, :],
                                         start=(c == 0), stop=False)
                    for c in range(DC):
                        last = nc.tensor.matmul(bank_d0[:, b * D + c * P:b * D + (c + 1) * P], o_t[:, c, rows],
                                                ident[:, :], is_transpose=True, start=False, stop=(c == DC - 1))
                last.then_inc(ff2_out, 1)

            def turn(u):
                a, b, c, d = u.a, u.b, u.c, u.d
                if a: a_transpose(a)
                if b: b_transpose(b)
                if c: c_transpose(c)
                if a: a_project(a)
                if b: b_project(b)
                if d: d_project(d, 0)
                if c: c_sd(c)
                if c: c_scores(c, 0)
                if d: d_project(d, 1)
                if a: a_scores(a)
                if b: b_scores(b)
                if c: c_project(c, 0)
                if d: d_scores(d)
                if c: c_project(c, 1)
                if a: a_turn(a)
                if b: b_turn(b)
                if c: c_scores(c, 1)
                if c: c_project(c, 2)
                if d: d_turn(d)
                if a: a_mix(a)
                if b: b_mix(b)
                if c: c_project(c, 3)
                if d: d_mix(d)
                if c: c_turn(c, 0)
                if b: b_convolve(b)
                if d: d_ff1(d)
                if c: c_turn(c, 1)
                if c: c_mix(c, 0)
                if c: c_mix(c, 1)
                if d: d_ff2(d)
                if b: b_conv_project(b)
                if c: c_mix(c, 2)
                if c: c_mix(c, 3)

            def weights(t):
                if t == 0:
                    pe.wait_ge(w1_lo, 1)
                    pe.wait_ge(w2_in, 16)
                if t == 1:
                    pe.wait_ge(wh_lo, 2)
                if t == 2:
                    pe.wait_ge(attended, WO_COLUMNS)
                    pe.wait_ge(wo_in, 16)
                    pe.wait_ge(ff_in, 32)

            pe.wait_ge(made, 4)
            pe.wait_ge(ident_made, 1)
            pe.wait_ge(adj_made, 7)
            pe.wait_ge(w0_lo, 1)
            run_turns(pe, turn, weights)

        @block.scalar
        def _(act):
            def flat(t):
                return t[:, :, :, :].rearrange("p a b c -> p (a b c)")

            def exps(att, s):
                act.wait_ge(att.biased, s.n)
                for b in range(G):
                    z = att.scores[:, b * P:(b + 1) * P]
                    nc.scalar.activation(att.e1[:, b, :], z, ACT.Exp, bias=att.bias[:, 0, b:b + 1])
                    last = nc.scalar.activation(att.e2[:, b, :], z, ACT.Exp, bias=att.bias[:, 1, b:b + 1],
                                                scale=att.slope)
                last.then_inc(att.expd, 1)

            def keep_weights(att, s):
                act.wait_ge(att.turned, s.n)
                nc.scalar.copy(att.p_t[:, :, :].rearrange("p b n -> p (b n)"), att.probs[:, 0:G * P])\
                    .then_inc(att.kept, 1)

            def high(src_bank, dst, arrived, done, s):
                act.wait_ge(arrived, s.n)
                nc.scalar.copy(flat(dst), src_bank[:, :]).then_inc(done, 1)

            def exps3(s, b):
                act.wait_ge(biased3[b], s.n)
                for h in range(H):
                    z = bank_c0[:, h * P:(h + 1) * P]
                    nc.scalar.activation(e13[:, b, h, :], z, ACT.Exp, bias=bias3[:, b, 0, h:h + 1])
                    last = nc.scalar.activation(e23[:, b, h, :], z, ACT.Exp, bias=bias3[:, b, 1, h:h + 1],
                                                scale=SLOPE_L3)
                last.then_inc(expd3[b], 1)

            def keep_head_proj(s, k):
                act.wait_ge(head_proj[k], s.n)
                nc.scalar.copy(proj3[:, k // 2, (k % 2) * 512:(k % 2 + 1) * 512], bank_c1[:, :])\
                    .then_inc(head_proj_kept[k], 1)

            def keep_weights3(s, b):
                act.wait_ge(turned3[b], s.n)
                nc.scalar.copy(p3_t[:, b, :, :].rearrange("p h n -> p (h n)"), (bank_c0, bank_c1)[b][:, :])\
                    .then_inc(kept3[b], 1)

            def elu_exp(s, h):
                act.wait_ge(mixed3[h], s.n)
                nc.scalar.activation(elu3[:, h % 2, :], (bank_c0, bank_c1)[h % 2][:, :], ACT.Exp)\
                    .then_inc(elu_exp3[h], 1)

            def turn(u):
                a, b, c, d = u.a, u.b, u.c, u.d
                if a: high(bank_a0, xt0_h, xt0, hi0, a)
                if b: high(bank_b0, xt1_h, xt1, hi1, b)
                if c: high(bank_c0, xt3_h, xt3, hi3, c)
                if a:
                    for g, src in enumerate((bank_a0, bank_a1)):
                        act.wait_ge(projected0[g], a.n)
                        last = nc.scalar.copy(proj0[:, g, :], src[:, 0:D + 2])
                    last.then_inc(proj0_kept, 1)
                if b:
                    act.wait_ge(projected1, b.n)
                    nc.scalar.copy(proj1[:, :, :].rearrange("p b f -> p (b f)"), bank_b1[:, 0:G * (F1 + 2)])\
                        .then_inc(proj1_kept, 1)
                if d:
                    act.wait_ge(projected4[0], d.n)
                    nc.scalar.copy(proj4[:, 0, :], bank_d0[:, 0:D + 2])
                if c:
                    act.wait_ge(scored_c, c.n)
                    nc.scalar.copy(sd3[:, :, :].rearrange("p b k -> p (b k)"), bank_c1[:, 0:G * 2 * H])\
                        .then_inc(sd_kept, 1)
                    exps3(c, 0)
                if d:
                    act.wait_ge(projected4[1], d.n)
                    nc.scalar.copy(proj4[:, 1, :], bank_d1[:, 0:D + 2]).then_inc(proj4_kept, 1)
                if a: exps(att0, a)
                if b: exps(att1, b)
                if c: keep_head_proj(c, 0)
                if d: exps(att4, d)
                if c: keep_head_proj(c, 1)
                if a: keep_weights(att0, a)
                if b: keep_weights(att1, b)
                if c: exps3(c, 1)
                if c: keep_head_proj(c, 2)
                if d: keep_weights(att4, d)
                if c: keep_head_proj(c, 3)
                if d:
                    act.wait_ge(mixed4, d.n)
                    nc.scalar.activation(elu4[:, :], bank_d0[:, :], ACT.Exp).then_inc(elu_exp4, 1)
                if c: keep_weights3(c, 0)
                if b:
                    act.wait_ge(norm1.done, b.n)
                    nc.scalar.copy(x2_h[:, :, :], x2[:, :, :]).then_inc(x2_hi, 1)
                    act.wait_ge(conv[0], b.n)
                    nc.scalar.copy(conv_t[:, 0, :, :, :].rearrange("p c k n -> p (c k n)"), bank_b1[:, :])\
                        .then_inc(conv_kept[0], 1)
                if d:
                    act.wait_ge(ff1_out, d.n)
                    for m in range(DC):
                        last = nc.scalar.activation(relu_t[:, m, :], bank_d1[:, m * G * P:(m + 1) * G * P],
                                                    ACT.Relu, bias=fb1_c[:, m:m + 1])
                    last.then_inc(relu_ready, 1)
                if c: keep_weights3(c, 1)
                if c:
                    for h in range(H):
                        elu_exp(c, h)

            def split_weights(t):
                if t == 0:
                    act.wait_ge(attended, W1_COLUMNS)
                    act.wait_ge(w1_in, 16)
                    nc.scalar.copy(w1_h[:, :, :], w1_s[:, :, :]).then_inc(w1_hi, 1)
                if t == 1:
                    act.wait_ge(attended, WH_COLUMNS)
                    act.wait_ge(wh_in, 16 * H)
                    nc.scalar.copy(wh_h[:, :, :], wh_s[:, :, :]).then_inc(wh_hi, 1)
                    nc.scalar.copy(wa_h[:, :, :], wa_s[:, :, :]).then_inc(wh_hi, 1)

            act.wait_ge(made, 4)
            nc.scalar.copy(ident_r[:, :], ident[:, :]).then_inc(ident_made, 1)
            act.wait_ge(attended, W0_COLUMNS)
            act.wait_ge(w0_in, 16)
            nc.scalar.copy(w0_h[:, :, :], w0_s[:, :, :]).then_inc(w0_hi, 1)
            act.wait_ge(vec_in, 16 * 14)
            run_turns(act, turn, split_weights)

        @block.vector
        def _(dve):
            def flat(t):
                return t[:, :, :, :].rearrange("p a b c -> p (a b c)")

            def low(src_bank, hi, lo, hi_done, lo_done, s):
                dve.wait_ge(hi_done, s.n)
                nc.vector.tensor_tensor(flat(lo), src_bank[:, :], flat(hi).bitcast(F32), ALU.subtract)\
                    .then_inc(lo_done, 1)

            def biases(top, neg, neg_max, bias1, bias2, s_col, slope, z, sems, n):
                scored, maxing, biased = sems
                dve.wait_ge(scored, n)
                nc.vector.reduce_max(top, z, AX.X).then_inc(maxing, 1)
                dve.wait_ge(maxing, n * 3 - 2)
                nc.vector.scalar_tensor_tensor(neg, s_col, -1.0, top, ALU.mult, ALU.subtract).then_inc(maxing, 1)
                dve.wait_ge(maxing, n * 3 - 1)
                nc.vector.scalar_tensor_tensor(neg_max, neg, slope, neg, ALU.mult, ALU.min).then_inc(maxing, 1)
                dve.wait_ge(maxing, n * 3)
                nc.vector.scalar_tensor_tensor(bias1, s_col, 1.0, neg_max, ALU.mult, ALU.add)
                nc.vector.scalar_tensor_tensor(bias2, s_col, slope, neg_max, ALU.mult, ALU.add).then_inc(biased, 1)

            def att_biases(att, s):
                biases(att.top[:, :], att.neg[:, :], att.neg_max[:, :], att.bias[:, 0, :], att.bias[:, 1, :],
                       att.s.rearrange("p b k -> p (b k)"), att.slope,
                       att.scores[:, 0:G * P].rearrange("p (b n) -> p b n", b=G),
                       (att.scored, att.maxing, att.biased), s.n)

            def att_weights(att, s):
                dve.wait_ge(att.expd, s.n)
                for b in range(G):
                    last = nc.vector.scalar_tensor_tensor(att.p[:, b, :], att.e1[:, b, :], 1.0, att.e2[:, b, :],
                                                          ALU.mult, ALU.max, accum_out=att.sum[:, b:b + 1])
                last.then_inc(att.weighed, 1)
                dve.wait_ge(att.weighed, s.n)
                nc.vector.reciprocal(att.rsum[:, :], att.sum[:, :]).then_inc(att.inverted, 1)

            def biases3(s, b):
                biases(top3[:, b, :], neg3[:, b, :], neg_max3[:, b, :], bias3[:, b, 0, :], bias3[:, b, 1, :],
                       sd3[:, b, 0:H], SLOPE_L3, bank_c0[:, :].rearrange("p (h n) -> p h n", h=H),
                       (z3[b], maxing3[b], biased3[b]), s.n)

            def weights3(s, b):
                dve.wait_ge(expd3[b], s.n)
                for h in range(H):
                    last = nc.vector.scalar_tensor_tensor(p3[:, b, h, :], e13[:, b, h, :], 1.0, e23[:, b, h, :],
                                                          ALU.mult, ALU.max, accum_out=sum3[:, b, h:h + 1])
                last.then_inc(weighed3[b], 1)
                dve.wait_ge(weighed3[b], s.n)
                nc.vector.reciprocal(rsum3[:, b, :], sum3[:, b, :]).then_inc(inverted3[b], 1)

            def moments(norm, s):
                dve.wait_ge(norm.summed, s.n)
                for b in range(G):
                    last = nc.vector.bn_stats(norm.stats[:, b, :], norm.y[:, b, :])
                last.then_inc(norm.averaged, 1)
                dve.wait_ge(norm.averaged, s.n * 2 - 1)
                nc.vector.tensor_copy(junk[:, 0:1], eps_c[:, 0:1])
                for b in range(G):
                    last = nc.vector.bn_aggr(norm.moments[:, b, :], norm.stats[:, b, :])
                last.then_inc(norm.averaged, 1)

            def normed(norm, dst, s):
                dve.wait_ge(norm.scaled, s.n * 2)
                for b in range(G):
                    last = nc.vector.tensor_scalar(dst[:, b, :], norm.y[:, b, :], norm.moments[:, b, 0:1],
                                                   norm.rstd[:, b:b + 1], ALU.subtract, ALU.mult)
                last.then_inc(norm.done, 1)

            def elu(src_bank, low_tile, dst, exp_done, low_done, done, s):
                dve.wait_ge(exp_done, s.n)
                nc.vector.tensor_scalar(low_tile, low_tile, 1.0, 1.0, ALU.min, ALU.subtract).then_inc(low_done, 1)
                dve.wait_ge(low_done, s.n)
                nc.vector.tensor_tensor(dst, src_bank[:, :], low_tile, ALU.max).then_inc(done, 1)

            def head_elu(s, h):
                elu((bank_c0, bank_c1)[h % 2], elu3[:, h % 2, :],
                    h_t[:, h, :, :, :].rearrange("p c b n -> p (c b n)"), elu_exp3[h], elu_low3[h], h_ready[h], s)

            def turn(u):
                a, b, c, d = u.a, u.b, u.c, u.d
                if a: low(bank_a0, xt0_h, xt0_l, hi0, lo0, a)
                if b: low(bank_b0, xt1_h, xt1_l, hi1, lo1, b)
                if c: low(bank_c0, xt3_h, xt3_l, hi3, lo3, c)
                if c: biases3(c, 0)
                if a: att_biases(att0, a)
                if b: att_biases(att1, b)
                if c: weights3(c, 0)
                if d: att_biases(att4, d)
                if a:
                    att_weights(att0, a)
                    dve.wait_ge(att0.inverted, a.n)
                    nc.vector.tensor_scalar(att0.rsum[:, :], att0.rsum[:, :], has_neighbour[:, 0:1], None, ALU.mult)\
                        .then_inc(gated0, 1)
                if b: att_weights(att1, b)
                if c: biases3(c, 1)
                if d: att_weights(att4, d)
                if a:
                    dve.wait_ge(mixed0, a.n)
                    dve.wait_ge(gated0, a.n)
                    for g in range(G):
                        last = nc.vector.scalar_tensor_tensor(norm0.y[:, g, :], bank_a0[:, g * D:(g + 1) * D],
                                                              att0.rsum[:, g:g + 1], x0[:, g, :], ALU.mult, ALU.add)
                    last.then_inc(norm0.summed, 1)
                    moments(norm0, a)
                if b:
                    dve.wait_ge(mixed1, b.n)
                    dve.wait_ge(att1.inverted, b.n)
                    for g in range(G):
                        nc.vector.scalar_tensor_tensor(norm1.y[:, g, 0:F1], bank_b0[:, g * F1:(g + 1) * F1],
                                                       att1.rsum[:, g:g + 1], x1[:, g, 0:F1], ALU.mult, ALU.add)
                    nc.vector.tensor_tensor(norm1.y[:, :, F1:D], proj1[:, :, 0:F1], x1[:, :, F1:D], ALU.add)\
                        .then_inc(norm1.summed, 1)
                    moments(norm1, b)
                if a: normed(norm0, x1, a)
                if b: normed(norm1, x2, b)
                if c: weights3(c, 1)
                if d: elu(bank_d0, elu4[:, :], o_t[:, :, :].rearrange("p c n -> p (c n)"), elu_exp4, elu_low4,
                          o_ready, d)
                if b:
                    dve.wait_ge(conv[1], b.n)
                    nc.vector.tensor_copy(conv_t[:, 1, :, :, :].rearrange("p c k n -> p (c k n)"), bank_b0[:, :])\
                        .then_inc(conv_kept[1], 1)
                if c: head_elu(c, 0)
                if c: head_elu(c, 1)
                if d:
                    dve.wait_ge(ff2_out, d.n)
                    nc.vector.tensor_tensor(norm3.y[:, :, :], bank_d0[:, :].rearrange("p (b f) -> p b f", b=G),
                                            fb2_bc[:, :].unsqueeze(1).to_broadcast([P, G, D]), ALU.add)\
                        .then_inc(norm3.summed, 1)
                    moments(norm3, d)
                if b:
                    dve.wait_ge(conv_out, b.n)
                    dve.wait_ge(x2_biased, b.n)
                    nc.vector.tensor_tensor(norm2.y[:, :, :], bank_b1[:, :].rearrange("p (b f) -> p b f", b=G),
                                            x2_b[:, :, :], ALU.add).then_inc(norm2.summed, 1)
                    moments(norm2, b)
                if d: normed(norm3, n3, d)
                if c: head_elu(c, 2)
                if b:
                    if b.again:
                        dve.wait_ge(x3_biased, b.before)
                    normed(norm2, x3, b)
                if c: head_elu(c, 3)
                if d:
                    dve.wait_ge(scaled3, d.n)
                    dve.wait_ge(x3_biased, d.n)
                    nc.vector.tensor_tensor(norm4.y[:, :, :], n3_g[:, :, :],
                                            x3_b[:, bass.ds((u.t + 1) % 2 * G, G), :], ALU.add)\
                        .then_inc(norm4.summed, 1)
                    moments(norm4, d)
                    if d.again:
                        dve.wait_ge(stored, d.before * 16)
                    normed(norm4, result, d)

            columns = [0]

            def attend(w, a_vec, dst):
                if columns[0]:
                    dve.wait_ge(attended, columns[0])
                columns[0] += 1
                nc.vector.scalar_tensor_tensor(junk[:, 0:w.shape[1]], w, 1.0, a_vec, ALU.mult, ALU.mult,
                                               accum_out=dst).then_inc(attended, 1)

            def prepare(t):
                if t == 0:
                    for c in range(DC):
                        for k in range(2):
                            attend(w1_s[:, c, 0:F1], a1_bc[:, k, :], w1_s[:, c, F1 + k:F1 + k + 1])
                    dve.wait_ge(w1_hi, 1)
                    nc.vector.tensor_tensor(w1_l[:, :, :], w1_s[:, :, :], w1_h[:, :, :].bitcast(F32), ALU.subtract)\
                        .then_inc(w1_lo, 1)
                if t == 1:
                    dve.wait_ge(wh_in, 16 * H)
                    for c in range(DC):
                        for h in range(H):
                            for k in range(2):
                                attend(wh_s[:, c, h * D:(h + 1) * D], ah_bc[:, h, k, :],
                                       wa_s[:, c, k * H + h:k * H + h + 1])
                    dve.wait_ge(wh_hi, 2)
                    nc.vector.tensor_tensor(wh_l[:, :, :], wh_s[:, :, :], wh_h[:, :, :].bitcast(F32), ALU.subtract)\
                        .then_inc(wh_lo, 1)
                    nc.vector.tensor_tensor(wa_l[:, :, :], wa_s[:, :, :], wa_h[:, :, :].bitcast(F32), ALU.subtract)\
                        .then_inc(wh_lo, 1)
                if t == 2:
                    dve.wait_ge(wo_in, 16)
                    for k in range(HC):
                        for j in range(2):
                            attend(wo_s[:, k, 0:D], ao_bc[:, j, :], wo_s[:, k, D + j:D + j + 1])

            dve.wait_ge(adj_in, 32)
            nc.vector.tensor_scalar(mask[:, :], adj_i[:, :], 0.0, FAR, ALU.is_equal, ALU.mult).then_inc(adj_made, 1)
            nc.vector.tensor_scalar(nonzero[:, :], adj_i[:, :], 0.0, None, ALU.not_equal).then_inc(adj_made, 1)
            nc.vector.tensor_copy(adj_deg[:, 0, :], adj_ti[:, :]).then_inc(adj_made, 1)
            nc.vector.reduce_sum(degree[:, :], adj_i[:, :], AX.X).then_inc(adj_made, 1)
            dve.wait_ge(adj_made, 4)
            nc.vector.reduce_max(has_neighbour[:, :], nonzero[:, :], AX.X).then_inc(adj_made, 1)
            dve.wait_ge(made, 4)
            nc.vector.tensor_scalar(adj_deg[:, 1, :], ident[:, :], degree[:, 0:1], None, ALU.mult).then_inc(adj_made, 1)
            dve.wait_ge(vec_in, 16 * 14)
            nc.vector.tensor_scalar(deg_b[:, :], b2_bc[:, :], degree[:, 0:1], None, ALU.mult).then_inc(adj_made, 1)
            dve.wait_ge(adj_made, 7)
            dve.wait_ge(w0_in, 16)
            for c in range(DC):
                for k in range(2):
                    attend(w0_s[:, c, 0:D], a0_bc[:, k, :], w0_s[:, c, D + k:D + k + 1])
            dve.wait_ge(w0_hi, 1)
            nc.vector.tensor_tensor(w0_l[:, :, :], w0_s[:, :, :], w0_h[:, :, :].bitcast(F32), ALU.subtract)\
                .then_inc(w0_lo, 1)
            dve.wait_ge(w1_in, 16)
            run_turns(dve, turn, prepare)


def kernel(x, adj, L0_gnn_W, L0_gnn_a_src, L0_gnn_a_dst, L1_gnn_W, L1_gnn_a, L2_gnn_W, L2_gnn_b,
           L3_gnn_W_heads, L3_gnn_a_heads, L3_gnn_W_out, L3_gnn_a_out, L3_gnn_w1, L3_gnn_b1,
           L3_gnn_w2, L3_gnn_b2, L3_gnn_ln_gamma, L3_gnn_ln_beta):
    import concourse.bacc as bacc
    from concourse.bass_utils import run_bass_kernel_spmd

    arrays = {
        "x_in": x, "adj_in": adj, "adj_t_in": np.asarray(adj).T, "w0_in": L0_gnn_W,
        "a0_src_in": L0_gnn_a_src, "a0_dst_in": L0_gnn_a_dst, "w1_in": L1_gnn_W,
        "a1_in": np.asarray(L1_gnn_a).reshape(2, F1), "w2_t_in": np.asarray(L2_gnn_W).T, "b2_in": L2_gnn_b,
        "wh_in": L3_gnn_W_heads, "ah_in": L3_gnn_a_heads, "wo_in": L3_gnn_W_out, "ao_in": L3_gnn_a_out,
        "ff1_in": L3_gnn_w1, "fb1_t_in": np.asarray(L3_gnn_b1).reshape(DC, P).T, "ff2_in": L3_gnn_w2, "fb2_in": L3_gnn_b2,
        "gamma_in": L3_gnn_ln_gamma, "beta_in": L3_gnn_ln_beta,
    }
    arrays = {f"{k}_dram": np.ascontiguousarray(v) for k, v in arrays.items()}
    nc = bacc.Bacc("TRN2", target_bir_lowering=False, num_devices=1)
    args = [nc.dram_tensor(k, v.shape, mybir.dt.from_np(v.dtype), kind="ExternalInput").ap()
            for k, v in arrays.items()]
    out = nc.dram_tensor("out_dram", (B, N, D), F32, kind="ExternalOutput").ap()
    build(nc, *args, out)
    r = run_bass_kernel_spmd(nc, [arrays], core_ids=[0])
    return r.results[0]["out_dram"]
```

```python
import concourse.bass as bass
import concourse.mybir as mybir
import numpy as np
from contextlib import ExitStack

B, N, D = 64, 128, 256
G = 2
UNITS = B // G
P = 128
DC = D // P
F1 = 128
H = 4
HC = H * DC
SLOPE_L0, SLOPE_L1, SLOPE_L3 = 0.2, 0.2, 0.01
FAR = -2.0 ** 100
EPS = 1e-5

F32 = mybir.dt.float32
F32R = mybir.dt.float32r
I32 = mybir.dt.int32
ALU = mybir.AluOpType
ACT = mybir.ActivationFunctionType
AX = mybir.AxisListType


W0_COLUMNS = 2 * DC
W1_COLUMNS = W0_COLUMNS + 2 * DC
WH_COLUMNS = W1_COLUMNS + 2 * H * DC
WO_COLUMNS = WH_COLUMNS + 2 * HC
VECTORS = 14
ADJ_MADE = 7
HCOLS = 2 * H + H * D
THIRDS = 3
FILL = HCOLS // THIRDS
FILLS = G * THIRDS


class Stage:

    def __init__(self, n, looped):
        self.n = n
        self.before = n - 1
        self.two_before = n - 2
        self.again = looped or n > 1
        self.third = looped or n > 2


class Turn:

    def __init__(self, t, looped=False):
        self.t, self.looped = t, looped

    def has(self, lag):
        return self.looped or 0 <= self.t - lag < UNITS

    def at(self, lag, step, *which):
        if self.has(lag):
            step(Stage(self.t + (1 - lag), self.looped), *which)


LAST_LAG = 5
FIRST_LOOPED, LAST_LOOPED = LAST_LAG + 2, UNITS - 2


def run_turns(eng, body, between=None):
    for t in range(FIRST_LOOPED):
        body(Turn(t))
        if between:
            between(t)
    with eng.Fori(FIRST_LOOPED, LAST_LOOPED + 1) as t:
        body(Turn(t, looped=True))
    for t in range(LAST_LOOPED + 1, UNITS + LAST_LAG):
        body(Turn(t))


def build(nc, x, adj, adj_t, w0, a0_src, a0_dst, w1, a1, w2_t, b2, wh, ah, wo, ao,
          ff1, fb1_t, ff2, fb2, gamma, beta, out):
    ctx = ExitStack()
    with ctx:
        def sb(name, shape, dt=F32):
            return ctx.enter_context(nc.sbuf_tensor(name, shape, dt))

        def bank(name):
            return ctx.enter_context(nc.psum_tensor(name, [P, 512], F32))

        def sem(name):
            return ctx.enter_context(nc.semaphore(name))

        ident = sb("ident", [P, P])
        ident_r = sb("ident_r", [P, P], F32R)
        adj_i = sb("adj_i", [P, P], I32)
        adj_ti = sb("adj_ti", [P, P], I32)
        mask = sb("mask", [P, P], F32R)
        nonzero = sb("nonzero", [P, P])
        has_neighbour = sb("has_neighbour", [P, 1])
        degree = sb("degree", [P, 1])
        adj_deg = sb("adj_deg", [P, 2, P], F32R)
        deg_b = sb("deg_b", [P, D])
        eps_c = sb("eps_c", [P, G])
        zero_c = sb("zero_c", [P, G])
        half_c = sb("half_c", [P, G])
        tick = sb("tick", [P, G])
        fb2_bc = sb("fb2_bc", [P, D])
        gamma_bc = sb("gamma_bc", [P, D])
        beta_bc = sb("beta_bc", [P, D])
        fb1_c = sb("fb1_c", [P, DC])
        w0_s = sb("w0_s", [P, DC, D + 2])
        w0_h = sb("w0_h", [P, DC, D + 2], F32R)
        w0_l = sb("w0_l", [P, DC, D + 2], F32R)
        w1_s = sb("w1_s", [P, DC, F1 + 2])
        w2_h = sb("w2_h", [P, 2, DC, D], F32R)
        w2_l = sb("w2_l", [P, 2, DC, D], F32R)
        wh_h = sb("wh_h", [P, DC, HCOLS], F32R)
        wh_l = sb("wh_l", [P, DC, HCOLS], F32R)
        wo_h = sb("wo_h", [P, HC, D + 2], F32R)
        wo_l = sb("wo_l", [P, HC, D + 2], F32R)
        ff1_h = sb("ff1_h", [P, DC, D], F32R)
        ff1_l = sb("ff1_l", [P, DC, D], F32R)
        ff2_h = sb("ff2_h", [P, DC, D], F32R)
        ff2_l = sb("ff2_l", [P, DC, D], F32R)
        wha_s = sb("wha_s", [P, DC, 2 * H])
        woa_s = sb("woa_s", [P, HC, 2])

        banks = [[bank(f"bank_{s}{k}") for k in range(2)] for s in "abcd"]
        (bank_a0, bank_a1), (bank_b0, bank_b1), (bank_c0, bank_c1), (bank_d0, bank_d1) = banks

        class Attention:

            def __init__(self, name, slope, scores, probs, proj, width):
                self.slope = slope
                self.scores, self.probs = scores, probs
                self.proj = proj
                self.s = proj[:, :, width:width + 1]
                self.d = proj[:, :, width + 1:width + 2]
                self.top = sb(f"{name}_top", [P, G])
                self.neg = sb(f"{name}_neg", [P, G])
                self.neg_max = sb(f"{name}_neg_max", [P, G])
                self.bias = sb(f"{name}_bias", [P, 2, G])
                self.e1 = sb(f"{name}_e1", [P, G, P])
                self.e2 = sb(f"{name}_e2", [P, G, P])
                self.p = sb(f"{name}_p", [P, G, P])
                self.sum = sb(f"{name}_sum", [P, G])
                self.rsum = sb(f"{name}_rsum", [P, G])
                self.p_t = sb(f"{name}_p_t", [P, G, P])
                self.scored = sem(f"{name}_scored")
                self.maxing = sem(f"{name}_maxing")
                self.biased = sem(f"{name}_biased")
                self.expd = sem(f"{name}_expd")
                self.weighed = sem(f"{name}_weighed")
                self.inverted = sem(f"{name}_inverted")
                self.turned = sem(f"{name}_turned")
                self.kept = sem(f"{name}_kept")

        class Norm:

            def __init__(self, name, on_act=False):
                self.on_act = on_act
                self.raises = 3 if on_act else 2
                self.y = sb(f"{name}_y", [P, G, D])
                self.stats = sb(f"{name}_stats", [P, G, 6])
                self.moments = sb(f"{name}_moments", [P, G, 2])
                self.var_eps = sb(f"{name}_var_eps", [P, G])
                self.rstd = sb(f"{name}_rstd", [P, G])
                self.tick = sb(f"{name}_tick", [P, 1])
                self.shift = sb(f"{name}_shift", [P, 2, G])
                self.summed = sem(f"{name}_summed")
                self.averaged = sem(f"{name}_averaged")
                self.scaled = sem(f"{name}_scaled")
                self.done = sem(f"{name}_done")

        def flat(t):
            n = len(t.shape) - 1
            if n == 1:
                return t[:, :]
            if n == 2:
                return t[:, :, :].rearrange("p a b -> p (a b)")
            if n == 3:
                return t[:, :, :, :].rearrange("p a b c -> p (a b c)")
            return t[:, :, :, :, :].rearrange("p a b c d -> p (a b c d)")

        x0 = sb("x0", [P, G, D])
        xt0_h = sb("xt0_h", [P, DC, G, P], F32R)
        xt0_l = sb("xt0_l", [P, DC, G, P], F32R)
        proj0 = sb("proj0", [P, G, D + 2])
        x1 = sb("x1", [P, G, D])
        att0 = Attention("att0", SLOPE_L0, bank_a0, bank_a1, proj0, D)
        norm0 = Norm("norm0")
        xt1_s = sb("xt1_s", [P, DC, G, P])
        proj1 = sb("proj1", [P, G, F1 + 2])
        x2 = sb("x2", [P, G, D])
        x2_h = sb("x2_h", [P, G, D], F32R)
        x2_l = sb("x2_l", [P, G, D], F32R)
        x2_b = sb("x2_b", [P, G, D])
        conv_h = sb("conv_h", [P, G, DC, 2, P], F32R)
        conv_l = sb("conv_l", [P, G, DC, 2, P], F32R)
        att1 = Attention("att1", SLOPE_L1, bank_b0, bank_b1, proj1, F1)
        norm1, norm2 = Norm("norm1"), Norm("norm2")
        x3 = sb("x3", [P, G, D])
        xt3_h = sb("xt3_h", [P, DC, G, P], F32R)
        xt3_l = sb("xt3_l", [P, DC, G, P], F32R)
        proj3 = sb("proj3", [P, G, HCOLS])
        top3 = sb("top3", [P, G, H])
        neg3 = sb("neg3", [P, G, H])
        neg_max3 = sb("neg_max3", [P, G, H])
        bias3 = sb("bias3", [P, G, 2, H])
        e3 = sb("e3", [P, G, 2, H, P])
        p3 = sb("p3", [P, G, H, P])
        sum3 = sb("sum3", [P, G, H])
        rsum3 = sb("rsum3", [P, G, H])
        p3_t = sb("p3_t", [P, G, H, P])
        elu3 = sb("elu3", [P, 2, 512])
        h_s = sb("h_s", [P, H, DC, G, P])
        h_h = sb("h_h", [P, H, DC, G, P], F32R)
        h_l = sb("h_l", [P, H, DC, G, P], F32R)
        proj4 = sb("proj4", [P, G, D + 2])
        att4 = Attention("att4", SLOPE_L3, bank_d0, bank_d1, proj4, D)
        elu4 = sb("elu4", [P, 512])
        o_s = sb("o_s", [P, DC, G * P])
        o_h = sb("o_h", [P, DC, G * P], F32R)
        o_l = sb("o_l", [P, DC, G * P], F32R)
        relu_s = sb("relu_s", [P, DC, G * P])
        relu_h = sb("relu_h", [P, DC, G * P], F32R)
        relu_l = sb("relu_l", [P, DC, G * P], F32R)
        x3_b = sb("x3_b", [P, 2 * G, D])
        norm3, norm4 = Norm("norm3", on_act=True), Norm("norm4", on_act=True)
        n3 = sb("n3", [P, G, D])
        n3_g = sb("n3_g", [P, G, D])
        result = sb("result", [P, G, D])
        wh_s = h_s[:, :, :, :, :].rearrange("p h c b n -> p (h c b n)").rearrange("p (c f) -> p c f", c=DC)
        wo_s = e3[:, :, :, :, :].rearrange("p b k h n -> p (b k h n)").rearrange("p (c f) -> p c f", c=HC)
        w2_s = flat(p3).rearrange("p (k c f) -> p k c f", k=2, c=DC)
        ff_s = flat(p3_t).rearrange("p (k c f) -> p k c f", k=2, c=DC)
        ah_bc = flat(proj3)[:, 0:2 * H * D].rearrange("p (h k f) -> p h k f", h=H, k=2)
        ao_bc = flat(elu3)[:, 0:2 * D].rearrange("p (k f) -> p k f", k=2)
        junk = elu4[:, 0:D]
        a0_bc = flat(o_s).rearrange("p (k f) -> p k f", k=2)
        a1_bc = flat(relu_s)[:, 0:2 * F1].rearrange("p (k f) -> p k f", k=2)
        b2_bc = flat(n3)[:, 0:D]

        made = sem("made")
        ident_made = sem("ident_made")
        adj_in, vec_in = sem("adj_in"), sem("vec_in")
        w0_in, w1_in, w2_in = sem("w0_in"), sem("w1_in"), sem("w2_in")
        wh_in, wo_in, ff_in = sem("wh_in"), sem("wo_in"), sem("ff_in")
        adj_made = sem("adj_made")
        attended = sem("attended")
        weights_hi = sem("weights_hi")
        weights_lo = sem("weights_lo")
        x0_in = sem("x0_in")
        stored = sem("stored")
        xt0, xt1, xt3 = sem("xt0"), sem("xt1"), sem("xt3")
        hi0, hi3 = sem("hi0"), sem("hi3")
        lo0, lo3 = sem("lo0"), sem("lo3")
        xt1_kept = sem("xt1_kept")
        projected0 = sem("projected0")
        projected1 = sem("projected1")
        proj0_kept, proj1_kept = sem("proj0_kept"), sem("proj1_kept")
        gated0 = sem("gated0")
        mixed0, mixed1 = sem("mixed0"), sem("mixed1")
        summed1b = sem("summed1b")
        x2_hi, x2_lo, x2_biased = sem("x2_hi"), sem("x2_lo"), sem("x2_biased")
        conv = sem("conv")
        conv_hi, conv_lo = sem("conv_hi"), sem("conv_lo")
        conv_out = sem("conv_out")
        x3_biased = sem("x3_biased")
        head_proj, head_proj_kept = sem("head_proj"), sem("head_proj_kept")
        z3 = sem("z3")
        maxing3 = sem("maxing3")
        biased3, expd3 = sem("biased3"), sem("expd3")
        weighed3, inverted3 = sem("weighed3"), sem("inverted3")
        normal3 = sem("normal3")
        turned3, kept3 = sem("turned3"), sem("kept3")
        mixed3 = sem("mixed3")
        elu_exp3, elu_low3 = sem("elu_exp3"), sem("elu_low3")
        h_made, h_hi, h_lo = sem("h_made"), sem("h_hi"), sem("h_lo")
        projected4, proj4_kept = sem("projected4"), sem("proj4_kept")
        normal4 = sem("normal4")
        mixed4, elu_exp4, elu_low4 = sem("mixed4"), sem("elu_exp4"), sem("elu_low4")
        o_made, o_hi, o_lo = sem("o_made"), sem("o_hi"), sem("o_lo")
        ff1_out, ff2_out = sem("ff1_out"), sem("ff2_out")
        relu_made, relu_hi, relu_lo = sem("relu_made"), sem("relu_hi"), sem("relu_lo")
        scaled3 = sem("scaled3")
        block = ctx.enter_context(nc.Block())

        @block.sync
        def _(sp):
            def unit(src, n):
                return src[bass.ds(n * G, G), :, :].rearrange("b n d -> n b d")

            sp.dma_start(adj_i[:, :], adj[:, :]).then_inc(adj_in, 16)
            sp.dma_start(adj_ti[:, :], adj_t[:, :]).then_inc(adj_in, 16)
            sp.dma_start(w0_s[:, :, 0:D], w0.rearrange("(c p) f -> p c f", p=P)).then_inc(w0_in, 16)
            sp.dma_start(x0[:, :, :], unit(x, 0)).then_inc(x0_in, 16)
            sp.dma_start(w1_s[:, :, 0:F1], w1.rearrange("(c p) f -> p c f", p=P)).then_inc(w1_in, 16)
            sp.dma_start(w2_s, w2_t.rearrange("(k c p) f -> p k c f", k=2, p=P)).then_inc(w2_in, 16)
            for h in range(H):
                sp.dma_start(wh_s[:, :, h * D:(h + 1) * D],
                             wh[h, :, :].rearrange("(c p) f -> p c f", p=P)).then_inc(wh_in, 16)
            sp.dma_start(wo_s, wo.rearrange("(c p) f -> p c f", p=P)).then_inc(wo_in, 16)
            sp.dma_start(ff_s[:, 0, :, :], ff1.rearrange("(c p) f -> p c f", p=P)).then_inc(ff_in, 16)
            sp.dma_start(ff_s[:, 1, :, :], ff2.rearrange("(c p) f -> p c f", p=P)).then_inc(ff_in, 16)

            def load_next(s):
                sp.wait_ge(norm0.summed, s.n)
                sp.dma_start(x0[:, :, :], unit(x, s.n)).then_inc(x0_in, 16)

            def store(s):
                sp.wait_ge(norm4.done, s.n)
                sp.dma_start(unit(out, s.before), result[:, :, :]).then_inc(stored, 16)

            def turn(u):
                if u.looped or u.t + 1 < UNITS:
                    u.at(0, load_next)
                u.at(5, store)

            run_turns(sp, turn)
            sp.wait_ge(stored, 16 * UNITS)

        @block.gpsimd
        def _(pool):
            def over_rows(v):
                return v.rearrange("(a n) -> a n", a=1).to_broadcast([P, v.shape[0]])

            def variance_eps(s, norm):
                pool.wait_ge(norm.averaged, s.n * 2)
                if norm.on_act:
                    if s.again:
                        pool.wait_ge(norm.done, s.before)
                    pool.tensor_tensor(norm.shift[:, 0, :], zero_c[:, :], norm.moments[:, :, 0], ALU.subtract)
                pool.tensor_tensor(norm.var_eps[:, :], norm.moments[:, :, 1], eps_c[:, :], ALU.add)\
                    .then_inc(norm.scaled, 1)

            def rstd(s, norm):
                pool.wait_ge(norm.scaled, s.n * norm.raises - (norm.raises - 1))
                pool.tensor_tensor(norm.rstd[:, :], norm.var_eps[:, :], half_c[:, :], ALU.pow)\
                    .then_inc(norm.scaled, 1)

            def shift(s, norm):
                pool.wait_ge(norm.scaled, s.n * 3 - 1)
                pool.tensor_tensor(norm.shift[:, 1, :], norm.shift[:, 0, :], norm.rstd[:, :], ALU.mult)\
                    .then_inc(norm.scaled, 1)

            def b_second_half(s):
                pool.wait_ge(proj1_kept, s.n)
                if s.again:
                    pool.wait_ge(norm1.done, s.before)
                pool.tensor_tensor(norm1.y[:, :, F1:D], proj1[:, :, 0:F1], x1[:, :, F1:D], ALU.add)\
                    .then_inc(summed1b, 1)

            def b_low(s):
                pool.wait_ge(x2_hi, s.n)
                pool.tensor_tensor(x2_l[:, :, :], x2[:, :, :], x2_h[:, :, :].bitcast(F32), ALU.subtract)\
                    .then_inc(x2_lo, 1)

            def b_bias(s):
                pool.wait_ge(norm1.done, s.n)
                if s.again:
                    pool.wait_ge(norm2.summed, s.before)
                pool.tensor_tensor(x2_b[:, :, :], x2[:, :, :],
                                   deg_b[:, :].unsqueeze(1).to_broadcast([P, G, D]), ALU.add)\
                    .then_inc(x2_biased, 1)

            def c_bias(s):
                pool.wait_ge(norm2.done, s.n)
                if s.third:
                    pool.wait_ge(norm4.summed, s.two_before)
                if s.again:
                    pool.wait_ge(x3_biased, s.before)
                pool.tensor_tensor(tick[:, :], zero_c[:, :], eps_c[:, :], ALU.add)
                pool.tensor_tensor(x3_b[:, bass.ds(s.before % 2 * G, G), :], x3[:, :, :],
                                   beta_bc[:, :].unsqueeze(1).to_broadcast([P, G, D]), ALU.add)\
                    .then_inc(x3_biased, 1)

            def c_normalise(s, b):
                pool.wait_ge(inverted3, s.n * G - (G - 1 - b))
                pool.tensor_tensor(p3[:, b, :, :], p3[:, b, :, :],
                                   rsum3[:, b, :].unsqueeze(2).to_broadcast([P, H, P]), ALU.mult)\
                    .then_inc(normal3, 1)

            def c_head_low(s, h):
                pool.wait_ge(h_hi, s.n * H - (H - 1 - h))
                pool.tensor_tensor(h_l[:, h, :, :, :], h_s[:, h, :, :, :], h_h[:, h, :, :, :].bitcast(F32),
                                   ALU.subtract).then_inc(h_lo, 1)

            def d_normalise(s):
                pool.wait_ge(att4.inverted, s.n)
                pool.tensor_tensor(att4.p[:, :, :], att4.p[:, :, :],
                                   att4.rsum[:, :].unsqueeze(2).to_broadcast([P, G, P]), ALU.mult)\
                    .then_inc(normal4, 1)

            def d_output_low(s):
                pool.wait_ge(o_hi, s.n)
                pool.tensor_tensor(o_l[:, :, :], o_s[:, :, :], o_h[:, :, :].bitcast(F32), ALU.subtract)\
                    .then_inc(o_lo, 1)

            def d_relu_low(s):
                pool.wait_ge(relu_hi, s.n)
                pool.tensor_tensor(relu_l[:, :, :], relu_s[:, :, :], relu_h[:, :, :].bitcast(F32), ALU.subtract)\
                    .then_inc(relu_lo, 1)

            def d_gamma(s):
                pool.wait_ge(norm3.done, s.n)
                if s.again:
                    pool.wait_ge(norm4.summed, s.before)
                pool.tensor_tensor(n3_g[:, :, :], n3[:, :, :],
                                   gamma_bc[:, :].unsqueeze(1).to_broadcast([P, G, D]), ALU.mult)\
                    .then_inc(scaled3, 1)

            def turn(u):
                u.at(1, variance_eps, norm0)
                u.at(1, rstd, norm0)
                u.at(3, c_normalise, 1)
                u.at(3, c_bias)
                u.at(4, d_output_low)
                u.at(2, variance_eps, norm2)
                u.at(2, rstd, norm2)
                u.at(3, c_head_low, 0)
                u.at(4, d_relu_low)
                u.at(3, c_head_low, 1)
                u.at(3, c_head_low, 2)
                u.at(3, c_head_low, 3)
                u.at(1, b_second_half)
                u.at(5, variance_eps, norm4)
                u.at(5, rstd, norm4)
                u.at(4, variance_eps, norm3)
                u.at(1, variance_eps, norm1)
                u.at(1, rstd, norm1)
                u.at(5, shift, norm4)
                u.at(4, rstd, norm3)
                u.at(1, b_low)
                u.at(4, shift, norm3)
                u.at(1, b_bias)
                u.at(2, c_normalise, 0)
                u.at(3, d_normalise)
                u.at(4, d_gamma)

            pool.memset(ident[:, :], 0.0).then_inc(made, 1)
            pool.memset(eps_c[:, :], EPS).then_inc(made, 1)
            pool.memset(zero_c[:, :], 0.0).then_inc(made, 1)
            pool.memset(half_c[:, :], -0.5).then_inc(made, 1)
            pool.wait_ge(made, 4)
            pool.affine_select(out=ident[:, :], in_=ident[:, :], compare_op=ALU.not_equal, fill=1.0, base=0,
                               pattern=[[-1, P]], channel_multiplier=1).then_inc(made, 1)
            for dst, src in ((a0_bc[:, 0, :], a0_src), (a0_bc[:, 1, :], a0_dst), (a1_bc[:, 0, :], a1[0, :]),
                             (a1_bc[:, 1, :], a1[1, :]), (b2_bc, b2), (fb2_bc[:, :], fb2),
                             (gamma_bc[:, :], gamma), (beta_bc[:, :], beta)):
                pool.dma_start(dst, over_rows(src)).then_inc(vec_in, 16)
            for h in range(H):
                pool.dma_start(ah_bc[:, h, :, :].rearrange("p k f -> p (k f)"), over_rows(ah[h, :]))\
                    .then_inc(vec_in, 16)
            pool.dma_start(ao_bc.rearrange("p k f -> p (k f)"), over_rows(ao)).then_inc(vec_in, 16)
            pool.dma_start(fb1_c[:, :], fb1_t[:, :]).then_inc(vec_in, 16)
            pool.wait_ge(adj_made, ADJ_MADE)
            pool.wait_ge(vec_in, 16 * VECTORS)
            run_turns(pool, turn)

        @block.tensor
        def _(pe):
            def transpose_x(src, dst):
                for c in range(DC):
                    for b in range(G):
                        k = c * G + b
                        last = nc.tensor.transpose(dst[:, k * P:(k + 1) * P], src[:, b, c * P:(c + 1) * P],
                                                   ident[:, :])
                return last

            def product(dst, pairs, open_end=False):
                for k, (left, right) in enumerate(pairs):
                    last = nc.tensor.matmul(dst, left, right, start=(k == 0),
                                            stop=(k == len(pairs) - 1 and not open_end))
                return last

            def parts(left_h, left_l, right_h, right_l, chunks):
                return [(left(c), right(c)) for left, right in ((left_l, right_h), (left_h, right_l),
                                                                (left_h, right_h)) for c in chunks]

            def scores(s, att):
                nc.tensor.matmul(att.scores[:, 0:G * P], ident_r[:, :],
                                 mask[:, :].unsqueeze(1).to_broadcast([P, G, P]), start=True, stop=False)
                for b in range(G):
                    last = nc.tensor.matmul(att.scores[:, b * P:(b + 1) * P],
                                            att.d[:, b, :].to_broadcast([P, P]), ident[:, :],
                                            is_transpose=True, start=False, stop=(b == G - 1))
                last.then_inc(att.scored, 1)

            def turn_weights(s, att):
                for b in range(G):
                    last = nc.tensor.transpose(att.probs[:, b * P:(b + 1) * P], att.p[:, b, :], ident[:, :])
                last.then_inc(att.turned, 1)

            def a_transpose(s):
                pe.wait_ge(x0_in, s.n * 16)
                if s.again:
                    pe.wait_ge(norm0.summed, s.before)
                transpose_x(x0, bank_a0).then_inc(xt0, 1)

            def a_project(s):
                if not s.again:
                    pe.wait_ge(weights_lo, 1)
                pe.wait_ge(lo0, s.n)
                for b, dst in enumerate((bank_a0, bank_a1)):
                    product(dst[:, 0:D + 2], parts(lambda c: xt0_h[:, c, b, :], lambda c: xt0_l[:, c, b, :],
                                                   lambda c: w0_h[:, c, :], lambda c: w0_l[:, c, :], range(DC)))\
                        .then_inc(projected0, 1)

            def a_scores(s):
                pe.wait_ge(proj0_kept, s.n)
                scores(s, att0)

            def a_turn(s):
                pe.wait_ge(att0.weighed, s.n)
                turn_weights(s, att0)

            def a_mix(s):
                pe.wait_ge(att0.kept, s.n)
                for b in range(G):
                    last = product(bank_a0[:, b * D:(b + 1) * D], [(att0.p_t[:, b, :], proj0[:, b, 0:D])])
                last.then_inc(mixed0, 1)

            def b_transpose(s):
                pe.wait_ge(norm0.done, s.n)
                if s.again:
                    pe.wait_ge(conv_lo, s.before * G)
                transpose_x(x1, bank_b0).then_inc(xt1, 1)

            def b_project(s):
                if not s.again:
                    pe.wait_ge(attended, W1_COLUMNS)
                    pe.wait_ge(w1_in, 16)
                pe.wait_ge(xt1_kept, s.n)
                if s.again:
                    pe.wait_ge(norm2.summed, s.before)
                for b in range(G):
                    last = product(bank_b1[:, b * (F1 + 2):(b + 1) * (F1 + 2)],
                                   [(xt1_s[:, c, b, :], w1_s[:, c, :]) for c in range(DC)])
                last.then_inc(projected1, 1)

            def b_scores(s):
                pe.wait_ge(proj1_kept, s.n)
                scores(s, att1)

            def b_turn(s):
                pe.wait_ge(att1.weighed, s.n)
                turn_weights(s, att1)

            def b_mix(s):
                pe.wait_ge(att1.kept, s.n)
                for b in range(G):
                    last = product(bank_b0[:, b * F1:(b + 1) * F1], [(att1.p_t[:, b, :], proj1[:, b, 0:F1])])
                last.then_inc(mixed1, 1)

            def b_convolve(s, b):
                if b == 0:
                    pe.wait_ge(x2_lo, s.n)
                else:
                    pe.wait_ge(norm1.summed, s.n)
                for c in range(DC):
                    last = product((bank_b1, bank_b0)[b][:, c * 2 * P:(c + 1) * 2 * P],
                                   [(part[:, b, c * P:(c + 1) * P], adj_deg[:, :, :]) for part in (x2_l, x2_h)])
                last.then_inc(conv, 1)

            def b_conv_project(s, b):
                if not s.again and b == 0:
                    pe.wait_ge(weights_lo, 2)
                pe.wait_ge(conv_lo, s.n * G - (G - 1 - b))
                last = product(bank_b1[:, b * D:(b + 1) * D],
                               parts(lambda k: conv_h[:, b, k[0], k[1], :], lambda k: conv_l[:, b, k[0], k[1], :],
                                     lambda k: w2_h[:, 1 - k[1], k[0], :], lambda k: w2_l[:, 1 - k[1], k[0], :],
                                     [(c, k) for c in range(DC) for k in range(2)]))
                if b == G - 1:
                    last.then_inc(conv_out, 1)

            def c_transpose(s):
                if not s.again:
                    pe.wait_ge(weights_lo, 6)
                pe.wait_ge(norm2.done, s.n)
                if s.again:
                    pe.wait_ge(h_made, s.before * H - 1)
                transpose_x(x3, bank_c0).then_inc(xt3, 1)

            def c_project(s, k):
                if k == 0:
                    pe.wait_ge(lo3, s.n)
                    if s.again:
                        pe.wait_ge(h_made, s.before * H)
                else:
                    pe.wait_ge(head_proj_kept, s.n * FILLS - (FILLS - k))
                b, cols = k // THIRDS, slice(k % THIRDS * FILL, (k % THIRDS + 1) * FILL)
                product(bank_c1[:, 0:FILL],
                        parts(lambda c: xt3_h[:, c, b, :], lambda c: xt3_l[:, c, b, :],
                              lambda c: wh_h[:, c, cols], lambda c: wh_l[:, c, cols], range(DC)))\
                    .then_inc(head_proj, 1)

            def c_scores(s, b):
                pe.wait_ge(head_proj_kept, s.n * FILLS - (FILLS - 1 - THIRDS * b))
                if b:
                    pe.wait_ge(expd3, s.n * G - 1)
                nc.tensor.matmul(bank_c0[:, :], ident_r[:, :], mask[:, :].unsqueeze(1).to_broadcast([P, H, P]),
                                 start=True, stop=False)
                for h in range(H):
                    last = nc.tensor.matmul(bank_c0[:, h * P:(h + 1) * P],
                                            proj3[:, b, H + h:H + h + 1].to_broadcast([P, P]), ident[:, :],
                                            is_transpose=True, start=False, stop=(h == H - 1))
                last.then_inc(z3, 1)

            def c_turn(s, b):
                pe.wait_ge(normal3, s.n * G - (G - 1 - b))
                if b == 0:
                    pe.wait_ge(expd3, s.n * G)
                else:
                    pe.wait_ge(head_proj_kept, s.n * FILLS)
                for h in range(H):
                    last = nc.tensor.transpose((bank_c0, bank_c1)[b][:, h * P:(h + 1) * P], p3[:, b, h, :],
                                               ident[:, :])
                last.then_inc(turned3, 1)

            def c_mix(s, h):
                if h < 2:
                    pe.wait_ge(kept3, s.n * G)
                else:
                    pe.wait_ge(h_made, s.n * H - (H + 1 - h))
                for c in range(DC):
                    for b in range(G):
                        k, f = c * G + b, 2 * H + h * D + c * P
                        last = product((bank_c0, bank_c1)[h % 2][:, k * P:(k + 1) * P],
                                       [(proj3[:, b, f:f + P], p3_t[:, b, h, :])])
                last.then_inc(mixed3, 1)

            def d_project(s, b):
                if b == 0:
                    pe.wait_ge(h_lo, s.n * H)
                    if s.again:
                        pe.wait_ge(norm3.summed, s.before)
                elif s.again:
                    pe.wait_ge(relu_made, s.before)
                product((bank_d0, bank_d1)[b][:, 0:D + 2],
                        parts(lambda k: h_h[:, k // DC, k % DC, b, :], lambda k: h_l[:, k // DC, k % DC, b, :],
                              lambda k: wo_h[:, k, :], lambda k: wo_l[:, k, :], range(HC)))\
                    .then_inc(projected4, 1)

            def d_scores(s):
                pe.wait_ge(proj4_kept, s.n * G)
                scores(s, att4)

            def d_turn(s):
                pe.wait_ge(normal4, s.n)
                turn_weights(s, att4)

            def d_mix(s):
                pe.wait_ge(att4.kept, s.n)
                for c in range(DC):
                    for b in range(G):
                        k = c * G + b
                        last = product(bank_d0[:, k * P:(k + 1) * P],
                                       [(proj4[:, b, c * P:(c + 1) * P], att4.p_t[:, b, :])])
                last.then_inc(mixed4, 1)

            def d_ff1(s):
                pe.wait_ge(o_lo, s.n)
                for m in range(DC):
                    cols = slice(m * P, (m + 1) * P)
                    last = product(bank_d1[:, m * G * P:(m + 1) * G * P],
                                   parts(lambda c: ff1_h[:, c, cols], lambda c: ff1_l[:, c, cols],
                                         lambda c: o_h[:, c, :], lambda c: o_l[:, c, :], range(DC)))
                last.then_inc(ff1_out, 1)

            def d_ff2(s):
                pe.wait_ge(relu_lo, s.n)
                for b in range(G):
                    rows = slice(b * P, (b + 1) * P)
                    product(bank_d0[:, b * D:(b + 1) * D],
                            parts(lambda c: relu_h[:, c, rows], lambda c: relu_l[:, c, rows],
                                  lambda c: ff2_h[:, c, :], lambda c: ff2_l[:, c, :], range(DC)), open_end=True)
                    for c in range(DC):
                        last = nc.tensor.matmul(bank_d0[:, b * D + c * P:b * D + (c + 1) * P], o_s[:, c, rows],
                                                ident[:, :], is_transpose=True, start=False, stop=(c == DC - 1))
                last.then_inc(ff2_out, 1)

            def turn(u):
                u.at(3, c_project, 5)
                u.at(3, c_turn, 0)
                u.at(4, d_mix)
                u.at(2, b_conv_project, 1)
                u.at(3, c_turn, 1)
                u.at(1, b_transpose)
                u.at(0, a_transpose)
                u.at(3, c_mix, 0)
                u.at(1, b_project)
                u.at(3, c_mix, 1)
                u.at(4, d_ff1)
                u.at(3, c_mix, 2)
                u.at(1, b_scores)
                u.at(3, c_mix, 3)
                u.at(0, a_project)
                u.at(2, c_transpose)
                u.at(4, d_ff2)
                u.at(1, b_turn)
                u.at(2, c_project, 0)
                u.at(0, a_scores)
                u.at(1, b_mix)
                u.at(2, c_scores, 0)
                u.at(2, c_project, 1)
                u.at(3, d_project, 0)
                u.at(2, c_project, 2)
                u.at(3, d_project, 1)
                u.at(2, c_project, 3)
                u.at(3, d_scores)
                u.at(1, b_convolve, 0)
                u.at(2, c_scores, 1)
                u.at(0, a_turn)
                u.at(1, b_convolve, 1)
                u.at(2, c_project, 4)
                u.at(0, a_mix)
                u.at(1, b_conv_project, 0)
                u.at(3, d_turn)

            pe.wait_ge(made, 5)
            pe.wait_ge(ident_made, 1)
            pe.wait_ge(adj_made, ADJ_MADE)
            run_turns(pe, turn)

        @block.scalar
        def _(act):
            def exps(s, att):
                act.wait_ge(att.biased, s.n)
                for b in range(G):
                    z = att.scores[:, b * P:(b + 1) * P]
                    nc.scalar.activation(att.e1[:, b, :], z, ACT.Exp, bias=att.bias[:, 0, b:b + 1])
                    last = nc.scalar.activation(att.e2[:, b, :], z, ACT.Exp, bias=att.bias[:, 1, b:b + 1],
                                                scale=att.slope)
                last.then_inc(att.expd, 1)

            def keep_weights(s, att):
                act.wait_ge(att.turned, s.n)
                nc.scalar.copy(flat(att.p_t), att.probs[:, 0:G * P]).then_inc(att.kept, 1)

            def norm_apply(s, norm, dst):
                act.wait_ge(norm.scaled, s.n * 3)
                for b in range(G):
                    last = nc.scalar.activation(dst[:, b, :], norm.y[:, b, :], ACT.Identity,
                                                bias=norm.shift[:, 1, b:b + 1], scale=norm.rstd[:, b:b + 1])
                last.then_inc(norm.done, 1)

            def a_high(s):
                act.wait_ge(xt0, s.n)
                if s.again:
                    act.wait_ge(projected0, s.before * G)
                nc.scalar.copy(flat(xt0_h), bank_a0[:, :]).then_inc(hi0, 1)

            def a_keep(s):
                if s.again:
                    act.wait_ge(mixed0, s.before)
                for b, src in enumerate((bank_a0, bank_a1)):
                    act.wait_ge(projected0, s.n * G - (G - 1 - b))
                    last = nc.scalar.copy(proj0[:, b, :], src[:, 0:D + 2])
                last.then_inc(proj0_kept, 1)

            def b_keep_x(s):
                act.wait_ge(xt1, s.n)
                if s.again:
                    act.wait_ge(projected1, s.before)
                nc.scalar.copy(flat(xt1_s), bank_b0[:, :]).then_inc(xt1_kept, 1)

            def b_keep(s):
                act.wait_ge(projected1, s.n)
                if s.again:
                    act.wait_ge(mixed1, s.before)
                    act.wait_ge(summed1b, s.before)
                nc.scalar.copy(flat(proj1), bank_b1[:, 0:G * (F1 + 2)]).then_inc(proj1_kept, 1)

            def b_high(s):
                act.wait_ge(norm1.done, s.n)
                if s.again:
                    act.wait_ge(conv, s.before * G)
                nc.scalar.copy(x2_h[:, :, :], x2[:, :, :]).then_inc(x2_hi, 1)

            def b_conv_high(s, b):
                act.wait_ge(conv, s.n * G - (G - 1 - b))
                if s.again and b == 0:
                    act.wait_ge(conv_out, s.before)
                nc.scalar.copy(conv_h[:, b, :, :, :].rearrange("p c k n -> p (c k n)"),
                               (bank_b1, bank_b0)[b][:, :]).then_inc(conv_hi, 1)

            def c_high(s):
                act.wait_ge(xt3, s.n)
                if s.again:
                    act.wait_ge(head_proj, s.before * FILLS)
                nc.scalar.copy(flat(xt3_h), bank_c0[:, :]).then_inc(hi3, 1)

            def c_keep(s, k):
                act.wait_ge(head_proj, s.n * FILLS - (FILLS - 1 - k))
                if s.again and k == 0:
                    act.wait_ge(mixed3, s.before * H)
                nc.scalar.copy(proj3[:, k // THIRDS, k % THIRDS * FILL:(k % THIRDS + 1) * FILL],
                               bank_c1[:, 0:FILL]).then_inc(head_proj_kept, 1)

            def c_exps(s, b):
                act.wait_ge(biased3, s.n * G - (G - 1 - b))
                for h in range(H):
                    z = bank_c0[:, h * P:(h + 1) * P]
                    nc.scalar.activation(e3[:, b, 0, h, :], z, ACT.Exp, bias=bias3[:, b, 0, h:h + 1])
                    last = nc.scalar.activation(e3[:, b, 1, h, :], z, ACT.Exp, bias=bias3[:, b, 1, h:h + 1],
                                                scale=SLOPE_L3)
                last.then_inc(expd3, 1)

            def c_keep_weights(s, b):
                act.wait_ge(turned3, s.n * G - (G - 1 - b))
                nc.scalar.copy(p3_t[:, b, :, :].rearrange("p h n -> p (h n)"), (bank_c0, bank_c1)[b][:, :])\
                    .then_inc(kept3, 1)

            def c_elu_exp(s, h):
                act.wait_ge(mixed3, s.n * H - (H - 1 - h))
                nc.scalar.activation(elu3[:, h % 2, :], (bank_c0, bank_c1)[h % 2][:, :], ACT.Exp)\
                    .then_inc(elu_exp3, 1)

            def c_head_high(s, h):
                act.wait_ge(h_made, s.n * H - (H - 1 - h))
                if s.again and h == 0:
                    act.wait_ge(projected4, s.before * G)
                nc.scalar.copy(h_h[:, h, :, :, :], h_s[:, h, :, :, :]).then_inc(h_hi, 1)

            def d_keep(s, b):
                act.wait_ge(projected4, s.n * G - (G - 1 - b))
                if s.again and b == 0:
                    act.wait_ge(mixed4, s.before)
                nc.scalar.copy(proj4[:, b, :], (bank_d0, bank_d1)[b][:, 0:D + 2]).then_inc(proj4_kept, 1)

            def d_elu_exp(s):
                act.wait_ge(mixed4, s.n)
                nc.scalar.activation(elu4[:, :], bank_d0[:, :], ACT.Exp).then_inc(elu_exp4, 1)

            def d_output_high(s):
                act.wait_ge(o_made, s.n)
                nc.scalar.copy(o_h[:, :, :], o_s[:, :, :]).then_inc(o_hi, 1)

            def d_relu(s):
                act.wait_ge(ff1_out, s.n)
                for m in range(DC):
                    last = nc.scalar.activation(relu_s[:, m, :], bank_d1[:, m * G * P:(m + 1) * G * P],
                                                ACT.Relu, bias=fb1_c[:, m:m + 1])
                last.then_inc(relu_made, 1)

            def d_relu_high(s):
                act.wait_ge(relu_made, s.n)
                nc.scalar.copy(relu_h[:, :, :], relu_s[:, :, :]).then_inc(relu_hi, 1)

            def d_norm3(s):
                if s.again:
                    act.wait_ge(scaled3, s.before)
                norm_apply(s, norm3, n3)

            def d_norm4(s):
                if s.again:
                    act.wait_ge(stored, s.before * 16)
                norm_apply(s, norm4, result)

            def turn(u):
                u.at(3, c_keep, 5)
                u.at(4, d_elu_exp)
                u.at(3, c_keep_weights, 0)
                u.at(3, c_keep_weights, 1)
                u.at(1, b_keep_x)
                u.at(4, d_output_high)
                u.at(3, c_elu_exp, 0)
                u.at(0, a_high)
                u.at(1, b_keep)
                u.at(3, c_elu_exp, 1)
                u.at(3, c_head_high, 0)
                u.at(4, d_relu)
                u.at(3, c_elu_exp, 2)
                u.at(4, d_relu_high)
                u.at(3, c_head_high, 1)
                u.at(3, c_elu_exp, 3)
                u.at(1, exps, att1)
                u.at(2, c_high)
                u.at(3, c_head_high, 2)
                u.at(0, a_keep)
                u.at(3, c_head_high, 3)
                u.at(1, keep_weights, att1)
                u.at(2, c_keep, 0)
                u.at(2, c_keep, 1)
                u.at(2, c_exps, 0)
                u.at(2, c_keep, 2)
                u.at(3, d_keep, 0)
                u.at(1, b_high)
                u.at(0, exps, att0)
                u.at(3, d_keep, 1)
                u.at(2, c_keep, 3)
                u.at(4, d_norm3)
                u.at(1, b_conv_high, 0)
                u.at(0, keep_weights, att0)
                u.at(3, exps, att4)
                u.at(1, b_conv_high, 1)
                u.at(2, c_keep, 4)
                u.at(2, c_exps, 1)
                u.at(3, keep_weights, att4)
                u.at(5, d_norm4)

            def weights(t):
                if t == 0:
                    act.wait_ge(w2_in, 16)
                    nc.scalar.copy(w2_h[:, :, :, :], w2_s).then_inc(weights_hi, 1)
                    act.wait_ge(attended, WH_COLUMNS)
                    act.wait_ge(wh_in, 16 * H)
                    nc.scalar.copy(wh_h[:, :, 0:2 * H], wha_s[:, :, :])
                    nc.scalar.copy(wh_h[:, :, 2 * H:HCOLS], wh_s).then_inc(weights_hi, 1)
                    act.wait_ge(attended, WO_COLUMNS)
                    act.wait_ge(wo_in, 16)
                    nc.scalar.copy(wo_h[:, :, D:D + 2], woa_s[:, :, :])
                    nc.scalar.copy(wo_h[:, :, 0:D], wo_s).then_inc(weights_hi, 1)
                    act.wait_ge(ff_in, 32)
                    nc.scalar.copy(ff1_h[:, :, :], ff_s[:, 0, :, :])
                    nc.scalar.copy(ff2_h[:, :, :], ff_s[:, 1, :, :]).then_inc(weights_hi, 1)

            act.wait_ge(made, 5)
            nc.scalar.copy(ident_r[:, :], ident[:, :]).then_inc(ident_made, 1)
            act.wait_ge(attended, W0_COLUMNS)
            act.wait_ge(w0_in, 16)
            nc.scalar.copy(w0_h[:, :, :], w0_s[:, :, :]).then_inc(weights_hi, 1)
            act.wait_ge(vec_in, 16 * VECTORS)
            run_turns(act, turn, weights)

        @block.vector
        def _(dve):
            def top(s, att):
                dve.wait_ge(att.scored, s.n)
                nc.vector.reduce_max(att.top[:, :], att.scores[:, 0:G * P].rearrange("p (b n) -> p b n", b=G), AX.X)\
                    .then_inc(att.maxing, 1)

            def s_of(att):
                return att.s.rearrange("p b k -> p (b k)")

            def neg(s, att):
                dve.wait_ge(att.maxing, s.n * 3 - 2)
                nc.vector.scalar_tensor_tensor(att.neg[:, :], s_of(att), -1.0, att.top[:, :],
                                               ALU.mult, ALU.subtract).then_inc(att.maxing, 1)

            def neg_max(s, att):
                dve.wait_ge(att.maxing, s.n * 3 - 1)
                nc.vector.scalar_tensor_tensor(att.neg_max[:, :], att.neg[:, :], att.slope, att.neg[:, :],
                                               ALU.mult, ALU.min).then_inc(att.maxing, 1)

            def biases(s, att):
                dve.wait_ge(att.maxing, s.n * 3)
                for k, factor in enumerate((1.0, att.slope)):
                    last = nc.vector.scalar_tensor_tensor(att.bias[:, k, :], s_of(att), factor,
                                                          att.neg_max[:, :], ALU.mult, ALU.add)
                last.then_inc(att.biased, 1)

            def weigh(s, att):
                dve.wait_ge(att.expd, s.n)
                for b in range(G):
                    last = nc.vector.scalar_tensor_tensor(att.p[:, b, :], att.e1[:, b, :], 1.0, att.e2[:, b, :],
                                                          ALU.mult, ALU.max, accum_out=att.sum[:, b:b + 1])
                last.then_inc(att.weighed, 1)

            def invert(s, att):
                dve.wait_ge(att.weighed, s.n)
                nc.vector.reciprocal(att.rsum[:, :], att.sum[:, :]).then_inc(att.inverted, 1)

            def statistics(s, norm):
                dve.wait_ge(norm.summed, s.n)
                for b in range(G):
                    last = nc.vector.bn_stats(norm.stats[:, b, :], norm.y[:, b, :])
                last.then_inc(norm.averaged, 1)

            def moments(s, norm):
                dve.wait_ge(norm.averaged, s.n * 2 - 1)
                nc.vector.tensor_copy(norm.tick[:, :], eps_c[:, 0:1])
                for b in range(G):
                    last = nc.vector.bn_aggr(norm.moments[:, b, :], norm.stats[:, b, :])
                last.then_inc(norm.averaged, 1)

            def norm_apply(s, norm, dst):
                dve.wait_ge(norm.scaled, s.n * 2)
                for b in range(G):
                    last = nc.vector.tensor_scalar(dst[:, b, :], norm.y[:, b, :], norm.moments[:, b, 0:1],
                                                   norm.rstd[:, b:b + 1], ALU.subtract, ALU.mult)
                last.then_inc(norm.done, 1)

            def a_low(s):
                dve.wait_ge(hi0, s.n)
                nc.vector.tensor_tensor(flat(xt0_l), bank_a0[:, :], flat(xt0_h).bitcast(F32), ALU.subtract)\
                    .then_inc(lo0, 1)

            def a_gate(s):
                dve.wait_ge(att0.inverted, s.n)
                nc.vector.tensor_scalar(att0.rsum[:, :], att0.rsum[:, :], has_neighbour[:, 0:1], None, ALU.mult)\
                    .then_inc(gated0, 1)

            def a_sum(s):
                dve.wait_ge(gated0, s.n)
                dve.wait_ge(mixed0, s.n)
                for b in range(G):
                    last = nc.vector.scalar_tensor_tensor(norm0.y[:, b, :], bank_a0[:, b * D:(b + 1) * D],
                                                          att0.rsum[:, b:b + 1], x0[:, b, :], ALU.mult, ALU.add)
                last.then_inc(norm0.summed, 1)

            def a_norm(s):
                if s.again:
                    dve.wait_ge(summed1b, s.before)
                    dve.wait_ge(norm1.summed, s.before)
                norm_apply(s, norm0, x1)

            def b_sum(s):
                dve.wait_ge(att1.inverted, s.n)
                dve.wait_ge(mixed1, s.n)
                for b in range(G):
                    last = nc.vector.scalar_tensor_tensor(norm1.y[:, b, 0:F1], bank_b0[:, b * F1:(b + 1) * F1],
                                                          att1.rsum[:, b:b + 1], x1[:, b, 0:F1], ALU.mult, ALU.add)
                last.then_inc(norm1.summed, 1)

            def b_statistics(s):
                dve.wait_ge(summed1b, s.n)
                statistics(s, norm1)

            def b_norm1(s):
                if s.again:
                    dve.wait_ge(x2_lo, s.before)
                    dve.wait_ge(x2_biased, s.before)
                norm_apply(s, norm1, x2)

            def b_conv_low(s, b):
                dve.wait_ge(conv_hi, s.n * G - (G - 1 - b))
                nc.vector.tensor_tensor(conv_l[:, b, :, :, :].rearrange("p c k n -> p (c k n)"),
                                        (bank_b1, bank_b0)[b][:, :],
                                        conv_h[:, b, :, :, :].rearrange("p c k n -> p (c k n)").bitcast(F32),
                                        ALU.subtract).then_inc(conv_lo, 1)

            def b_conv_sum(s):
                dve.wait_ge(x2_biased, s.n)
                dve.wait_ge(conv_out, s.n)
                nc.vector.tensor_tensor(norm2.y[:, :, :], bank_b1[:, :].rearrange("p (b f) -> p b f", b=G),
                                        x2_b[:, :, :], ALU.add).then_inc(norm2.summed, 1)

            def b_norm2(s):
                if s.again:
                    dve.wait_ge(x3_biased, s.before)
                    dve.wait_ge(xt3, s.before)
                norm_apply(s, norm2, x3)

            def c_low(s):
                dve.wait_ge(hi3, s.n)
                nc.vector.tensor_tensor(flat(xt3_l), bank_c0[:, :], flat(xt3_h).bitcast(F32), ALU.subtract)\
                    .then_inc(lo3, 1)

            def c_top(s, b):
                dve.wait_ge(z3, s.n * G - (G - 1 - b))
                nc.vector.reduce_max(top3[:, b, :], bank_c0[:, :].rearrange("p (h n) -> p h n", h=H), AX.X)\
                    .then_inc(maxing3, 1)

            def c_neg(s, b):
                dve.wait_ge(maxing3, s.n * 6 - (5 - 3 * b))
                nc.vector.scalar_tensor_tensor(neg3[:, b, :], proj3[:, b, 0:H], -1.0, top3[:, b, :],
                                               ALU.mult, ALU.subtract).then_inc(maxing3, 1)

            def c_neg_max(s, b):
                dve.wait_ge(maxing3, s.n * 6 - (4 - 3 * b))
                nc.vector.scalar_tensor_tensor(neg_max3[:, b, :], neg3[:, b, :], SLOPE_L3, neg3[:, b, :],
                                               ALU.mult, ALU.min).then_inc(maxing3, 1)

            def c_biases(s, b):
                dve.wait_ge(maxing3, s.n * 6 - (3 - 3 * b))
                for k, factor in enumerate((1.0, SLOPE_L3)):
                    last = nc.vector.scalar_tensor_tensor(bias3[:, b, k, :], proj3[:, b, 0:H], factor,
                                                          neg_max3[:, b, :], ALU.mult, ALU.add)
                last.then_inc(biased3, 1)

            def c_weigh(s, b):
                dve.wait_ge(expd3, s.n * G - (G - 1 - b))
                for h in range(H):
                    last = nc.vector.scalar_tensor_tensor(p3[:, b, h, :], e3[:, b, 0, h, :], 1.0, e3[:, b, 1, h, :],
                                                          ALU.mult, ALU.max, accum_out=sum3[:, b, h:h + 1])
                last.then_inc(weighed3, 1)

            def c_invert(s, b):
                dve.wait_ge(weighed3, s.n * G - (G - 1 - b))
                nc.vector.reciprocal(rsum3[:, b, :], sum3[:, b, :]).then_inc(inverted3, 1)

            def c_elu_low(s, h):
                dve.wait_ge(elu_exp3, s.n * H - (H - 1 - h))
                nc.vector.tensor_scalar(elu3[:, h % 2, :], elu3[:, h % 2, :], 1.0, 1.0, ALU.min, ALU.subtract)\
                    .then_inc(elu_low3, 1)

            def c_elu(s, h):
                dve.wait_ge(elu_low3, s.n * H - (H - 1 - h))
                if s.again:
                    dve.wait_ge(h_lo, s.before * H - (H - 1 - h))
                nc.vector.tensor_tensor(h_s[:, h, :, :, :].rearrange("p c b n -> p (c b n)"),
                                        (bank_c0, bank_c1)[h % 2][:, :], elu3[:, h % 2, :], ALU.max)\
                    .then_inc(h_made, 1)

            def d_elu_low(s):
                dve.wait_ge(elu_exp4, s.n)
                nc.vector.tensor_scalar(elu4[:, :], elu4[:, :], 1.0, 1.0, ALU.min, ALU.subtract)\
                    .then_inc(elu_low4, 1)

            def d_elu(s):
                dve.wait_ge(elu_low4, s.n)
                if s.again:
                    dve.wait_ge(ff2_out, s.before)
                nc.vector.tensor_tensor(flat(o_s), bank_d0[:, :], elu4[:, :], ALU.max).then_inc(o_made, 1)

            def d_sum3(s):
                dve.wait_ge(ff2_out, s.n)
                if s.again:
                    dve.wait_ge(norm3.done, s.before)
                nc.vector.tensor_tensor(norm3.y[:, :, :], bank_d0[:, :].rearrange("p (b f) -> p b f", b=G),
                                        fb2_bc[:, :].unsqueeze(1).to_broadcast([P, G, D]), ALU.add)\
                    .then_inc(norm3.summed, 1)

            def d_sum4(s):
                dve.wait_ge(x3_biased, s.n)
                if s.again:
                    dve.wait_ge(norm4.done, s.before)
                dve.wait_ge(scaled3, s.n)
                nc.vector.tensor_tensor(norm4.y[:, :, :], n3_g[:, :, :],
                                        x3_b[:, bass.ds(s.before % 2 * G, G), :], ALU.add)\
                    .then_inc(norm4.summed, 1)

            def turn(u):
                u.at(2, b_conv_low, 1)
                u.at(1, statistics, norm0)
                u.at(1, moments, norm0)
                u.at(3, c_weigh, 1)
                u.at(3, c_invert, 1)
                u.at(5, d_sum4)
                u.at(1, a_norm)
                u.at(4, d_elu_low)
                u.at(4, d_elu)
                u.at(2, b_conv_sum)
                u.at(5, statistics, norm4)
                u.at(2, statistics, norm2)
                u.at(3, c_elu_low, 0)
                u.at(2, moments, norm2)
                u.at(0, a_low)
                u.at(3, c_elu, 0)
                u.at(3, c_elu_low, 1)
                u.at(3, c_elu, 1)
                u.at(2, b_norm2)
                u.at(1, top, att1)
                u.at(3, c_elu_low, 2)
                u.at(1, neg, att1)
                u.at(1, neg_max, att1)
                u.at(3, c_elu, 2)
                u.at(1, biases, att1)
                u.at(3, c_elu_low, 3)
                u.at(3, c_elu, 3)
                u.at(1, weigh, att1)
                u.at(2, c_low)
                u.at(4, d_sum3)
                u.at(1, invert, att1)
                u.at(4, statistics, norm3)
                u.at(0, top, att0)
                u.at(0, neg, att0)
                u.at(5, moments, norm4)
                u.at(1, b_sum)
                u.at(0, neg_max, att0)
                u.at(2, c_top, 0)
                u.at(1, b_statistics)
                u.at(2, c_neg, 0)
                u.at(0, biases, att0)
                u.at(4, moments, norm3)
                u.at(1, moments, norm1)
                u.at(2, c_neg_max, 0)
                u.at(2, c_biases, 0)
                u.at(1, b_norm1)
                u.at(2, c_weigh, 0)
                u.at(0, weigh, att0)
                u.at(2, c_invert, 0)
                u.at(3, top, att4)
                u.at(0, invert, att0)
                u.at(3, neg, att4)
                u.at(3, neg_max, att4)
                u.at(3, biases, att4)
                u.at(2, c_top, 1)
                u.at(0, a_gate)
                u.at(2, c_neg, 1)
                u.at(2, c_neg_max, 1)
                u.at(1, b_conv_low, 0)
                u.at(2, c_biases, 1)
                u.at(3, weigh, att4)
                u.at(3, invert, att4)
                u.at(0, a_sum)

            columns = [0]

            def attend(w, a_vec, dst):
                if columns[0]:
                    dve.wait_ge(attended, columns[0])
                columns[0] += 1
                nc.vector.scalar_tensor_tensor(junk[:, 0:w.shape[1]], w, 1.0, a_vec, ALU.mult, ALU.mult,
                                               accum_out=dst).then_inc(attended, 1)

            def low(dst, src, hi):
                return nc.vector.tensor_tensor(dst, src, hi.bitcast(F32), ALU.subtract)

            def weights(t):
                if t == 0:
                    dve.wait_ge(w1_in, 16)
                    for c in range(DC):
                        for k in range(2):
                            attend(w1_s[:, c, 0:F1], a1_bc[:, k, :], w1_s[:, c, F1 + k:F1 + k + 1])
                    dve.wait_ge(wh_in, 16 * H)
                    for c in range(DC):
                        for h in range(H):
                            for k in range(2):
                                attend(wh_s[:, c, h * D:(h + 1) * D], ah_bc[:, h, k, :],
                                       wha_s[:, c, k * H + h:k * H + h + 1])
                    dve.wait_ge(wo_in, 16)
                    for k in range(HC):
                        for j in range(2):
                            attend(wo_s[:, k, :], ao_bc[:, j, :], woa_s[:, k, j:j + 1])
                    dve.wait_ge(weights_hi, 2)
                    low(w2_l[:, :, :, :], w2_s, w2_h[:, :, :, :]).then_inc(weights_lo, 1)
                    dve.wait_ge(weights_hi, 3)
                    low(wh_l[:, :, 0:2 * H], wha_s[:, :, :], wh_h[:, :, 0:2 * H])
                    low(wh_l[:, :, 2 * H:HCOLS], wh_s, wh_h[:, :, 2 * H:HCOLS]).then_inc(weights_lo, 1)
                    dve.wait_ge(weights_hi, 4)
                    low(wo_l[:, :, D:D + 2], woa_s[:, :, :], wo_h[:, :, D:D + 2])
                    low(wo_l[:, :, 0:D], wo_s, wo_h[:, :, 0:D]).then_inc(weights_lo, 1)
                    dve.wait_ge(weights_hi, 5)
                    low(ff1_l[:, :, :], ff_s[:, 0, :, :], ff1_h[:, :, :]).then_inc(weights_lo, 1)
                    low(ff2_l[:, :, :], ff_s[:, 1, :, :], ff2_h[:, :, :]).then_inc(weights_lo, 1)

            dve.wait_ge(adj_in, 32)
            nc.vector.tensor_scalar(mask[:, :], adj_i[:, :], 0.0, FAR, ALU.is_equal, ALU.mult).then_inc(adj_made, 1)
            nc.vector.tensor_scalar(nonzero[:, :], adj_i[:, :], 0.0, None, ALU.not_equal).then_inc(adj_made, 1)
            nc.vector.tensor_copy(adj_deg[:, 0, :], adj_ti[:, :]).then_inc(adj_made, 1)
            nc.vector.reduce_sum(degree[:, :], adj_i[:, :], AX.X).then_inc(adj_made, 1)
            dve.wait_ge(adj_made, 4)
            nc.vector.reduce_max(has_neighbour[:, :], nonzero[:, :], AX.X).then_inc(adj_made, 1)
            dve.wait_ge(made, 5)
            nc.vector.tensor_scalar(adj_deg[:, 1, :], ident[:, :], degree[:, 0:1], None, ALU.mult).then_inc(adj_made, 1)
            dve.wait_ge(vec_in, 16 * VECTORS)
            nc.vector.tensor_scalar(deg_b[:, :], b2_bc, degree[:, 0:1], None, ALU.mult).then_inc(adj_made, 1)
            dve.wait_ge(adj_made, ADJ_MADE)
            dve.wait_ge(w0_in, 16)
            for c in range(DC):
                for k in range(2):
                    attend(w0_s[:, c, 0:D], a0_bc[:, k, :], w0_s[:, c, D + k:D + k + 1])
            dve.wait_ge(weights_hi, 1)
            low(w0_l[:, :, :], w0_s[:, :, :], w0_h[:, :, :]).then_inc(weights_lo, 1)
            run_turns(dve, turn, weights)


def kernel(x, adj, L0_gnn_W, L0_gnn_a_src, L0_gnn_a_dst, L1_gnn_W, L1_gnn_a, L2_gnn_W, L2_gnn_b,
           L3_gnn_W_heads, L3_gnn_a_heads, L3_gnn_W_out, L3_gnn_a_out, L3_gnn_w1, L3_gnn_b1,
           L3_gnn_w2, L3_gnn_b2, L3_gnn_ln_gamma, L3_gnn_ln_beta):
    import concourse.bacc as bacc
    from concourse.bass_utils import run_bass_kernel_spmd

    arrays = {
        "x_in": x, "adj_in": adj, "adj_t_in": np.asarray(adj).T, "w0_in": L0_gnn_W,
        "a0_src_in": L0_gnn_a_src, "a0_dst_in": L0_gnn_a_dst, "w1_in": L1_gnn_W,
        "a1_in": np.asarray(L1_gnn_a).reshape(2, F1), "w2_t_in": np.asarray(L2_gnn_W).T, "b2_in": L2_gnn_b,
        "wh_in": L3_gnn_W_heads, "ah_in": L3_gnn_a_heads, "wo_in": L3_gnn_W_out, "ao_in": L3_gnn_a_out,
        "ff1_in": L3_gnn_w1, "fb1_t_in": np.asarray(L3_gnn_b1).reshape(DC, P).T, "ff2_in": L3_gnn_w2, "fb2_in": L3_gnn_b2,
        "gamma_in": L3_gnn_ln_gamma, "beta_in": L3_gnn_ln_beta,
    }
    arrays = {f"{k}_dram": np.ascontiguousarray(v) for k, v in arrays.items()}
    nc = bacc.Bacc("TRN2", target_bir_lowering=False, num_devices=1)
    args = [nc.dram_tensor(k, v.shape, mybir.dt.from_np(v.dtype), kind="ExternalInput").ap()
            for k, v in arrays.items()]
    out = nc.dram_tensor("out_dram", (B, N, D), F32, kind="ExternalOutput").ap()
    build(nc, *args, out)
    r = run_bass_kernel_spmd(nc, [arrays], core_ids=[0])
    return r.results[0]["out_dram"]
```

```python
import concourse.bass as bass
import concourse.mybir as mybir
import numpy as np
from contextlib import ExitStack

B, N, D = 64, 128, 256
G = 2
UNITS = B // G
P = 128
DC = D // P
F1 = 128
H = 4
HC = H * DC
SLOPE_L0, SLOPE_L1, SLOPE_L3 = 0.2, 0.2, 0.01
FAR = -2.0 ** 100
LOWEST = -2.0 ** 127
EPS = 1e-5

F32 = mybir.dt.float32
F32R = mybir.dt.float32r
I32 = mybir.dt.int32
ALU = mybir.AluOpType
ACT = mybir.ActivationFunctionType
AX = mybir.AxisListType


W0_COLUMNS = 2 * DC
W1_COLUMNS = W0_COLUMNS + 2 * DC
WH_COLUMNS = W1_COLUMNS + 2 * H * DC
WO_COLUMNS = WH_COLUMNS + 2 * HC
VECTORS = 4
ADJ_DEG, ADJ_MADE = 6, 7
W2_HI, WH_HI, FF_HI, WO_HI, WHA_HI, WOA_HI = 2, 3, 4, 5, 6, 7
W2_LO, FF_LO, WH_LO, WO_LO = 1, 2, 3, 4
HCOLS = 2 * H + H * D
THIRDS = 3
FILL = HCOLS // THIRDS
FILLS = G * THIRDS
FILL_ORDER = [(b, 0) for b in range(G)] + [(b, k) for b in range(G) for k in range(1, THIRDS)]


class Stage:

    def __init__(self, n, looped):
        self.n = n
        self.last = not looped and n == UNITS
        self.before = n - 1
        self.two_before = n - 2
        self.again = looped or n > 1
        self.third = looped or n > 2


class Turn:

    def __init__(self, t, looped=False):
        self.t, self.looped = t, looped

    def has(self, lag):
        return self.looped or 0 <= self.t - lag < UNITS

    def at(self, lag, step, *which):
        if self.has(lag):
            step(Stage(self.t + (1 - lag), self.looped), *which)


LAST_LAG = 7
UNROLL = 3
FIRST_LOOPED = LAST_LAG + 2
LAST_LOOPED = FIRST_LOOPED + (UNITS - 1 - FIRST_LOOPED) // UNROLL * UNROLL - 1


def run_turns(eng, body):
    for t in range(FIRST_LOOPED):
        body(Turn(t))
    with eng.Fori(FIRST_LOOPED, LAST_LOOPED + 2 - UNROLL, UNROLL) as t:
        for k in range(UNROLL):
            body(Turn(t + k, looped=True))
    for t in range(LAST_LOOPED + 1, UNITS + LAST_LAG):
        body(Turn(t))


def build(nc, x, x_t, adj, adj_t, w0, a0_src, a0_dst, w1, a1, w2_t, b2, wh, ah, wo, ao,
          ff1, fb1_t, ff2, fb2, gamma, beta, out):
    ctx = ExitStack()
    with ctx:
        def sb(name, shape, dt=F32):
            return ctx.enter_context(nc.sbuf_tensor(name, shape, dt))

        def bank(name):
            return ctx.enter_context(nc.psum_tensor(name, [P, 512], F32))

        def sem(name):
            return ctx.enter_context(nc.semaphore(name))

        ident = sb("ident", [P, P])
        adj_i = sb("adj_i", [P, P], I32)
        adj_ti = sb("adj_ti", [P, P], I32)
        mask = sb("mask", [P, P])
        nonzero = sb("nonzero", [P, P])
        has_neighbour = sb("has_neighbour", [P, 1])
        degree = sb("degree", [P, 1])
        adj_deg = sb("adj_deg", [P, 2, P], F32R)
        deg_b = sb("deg_b", [P, D])
        eps_c = sb("eps_c", [P, G])
        zero_c = sb("zero_c", [P, G])
        half_c = sb("half_c", [P, G])
        tick = sb("tick", [P, G])
        fb2_bc = sb("fb2_bc", [P, D])
        gamma_bc = sb("gamma_bc", [P, D])
        beta_bc = sb("beta_bc", [P, D])
        fb1_c = sb("fb1_c", [P, DC])
        w0_s = sb("w0_s", [P, DC, D + 2])
        w0_h = sb("w0_h", [P, DC, D + 2], F32R)
        w0_l = sb("w0_l", [P, DC, D + 2], F32R)
        w1_s = sb("w1_s", [P, DC, F1 + 2])
        w2_h = sb("w2_h", [P, 2, DC, D], F32R)
        w2_l = sb("w2_l", [P, 2, DC, D], F32R)
        wh_h = sb("wh_h", [P, DC, HCOLS], F32R)
        wh_l = sb("wh_l", [P, DC, HCOLS], F32R)
        wo_h = sb("wo_h", [P, HC, D + 2], F32R)
        wo_l = sb("wo_l", [P, HC, D + 2], F32R)
        ff1_h = sb("ff1_h", [P, DC, D], F32R)
        ff1_l = sb("ff1_l", [P, DC, D], F32R)
        ff2_h = sb("ff2_h", [P, DC, D], F32R)
        ff2_l = sb("ff2_l", [P, DC, D], F32R)
        wha_s = sb("wha_s", [P, DC, 2 * H])
        woa_s = sb("woa_s", [P, HC, 2])

        banks = [[bank(f"bank_{s}{k}") for k in range(2)] for s in "abcd"]
        (bank_a0, bank_a1), (bank_b0, bank_b1), (bank_c0, bank_c1), (bank_d0, bank_d1) = banks

        class Attention:

            def __init__(self, name, slope, scores, probs, proj, width):
                self.slope = slope
                self.scores, self.probs = scores, probs
                self.proj = proj
                self.s = proj[:, :, width:width + 1]
                self.d = proj[:, :, width + 1:width + 2]
                self.top = sb(f"{name}_top", [P, G])
                self.neg = sb(f"{name}_neg", [P, G])
                self.neg_max = sb(f"{name}_neg_max", [P, G])
                self.bias = sb(f"{name}_bias", [P, 2, G])
                self.tick = sb(f"{name}_tick", [P, 1])
                self.e1 = sb(f"{name}_e1", [P, G, P])
                self.e2 = sb(f"{name}_e2", [P, G, P])
                self.p = sb(f"{name}_p", [P, G, P])
                self.sum = sb(f"{name}_sum", [P, G])
                self.rsum = sb(f"{name}_rsum", [P, G])
                self.p_t = sb(f"{name}_p_t", [P, G, P])
                self.scored = sem(f"{name}_scored")
                self.maxing = sem(f"{name}_maxing")
                self.biased = sem(f"{name}_biased")
                self.expd = sem(f"{name}_expd")
                self.weighed = sem(f"{name}_weighed")
                self.inverted = sem(f"{name}_inverted")
                self.turned = sem(f"{name}_turned")
                self.kept = sem(f"{name}_kept")

        class Norm:

            def __init__(self, name, on_act=False):
                self.on_act = on_act
                self.raises = 3 if on_act else 2
                self.y = sb(f"{name}_y", [P, G, D])
                self.stats = sb(f"{name}_stats", [P, G, 6])
                self.moments = sb(f"{name}_moments", [P, G, 2])
                self.var_eps = sb(f"{name}_var_eps", [P, G])
                self.rstd = sb(f"{name}_rstd", [P, G])
                self.tick = sb(f"{name}_tick", [P, 1])
                self.shift = sb(f"{name}_shift", [P, 2, G])
                self.summed = sem(f"{name}_summed")
                self.averaged = sem(f"{name}_averaged")
                self.scaled = sem(f"{name}_scaled")
                self.done = sem(f"{name}_done")

        def flat(t):
            n = len(t.shape) - 1
            if n == 1:
                return t[:, :]
            if n == 2:
                return t[:, :, :].rearrange("p a b -> p (a b)")
            if n == 3:
                return t[:, :, :, :].rearrange("p a b c -> p (a b c)")
            return t[:, :, :, :, :].rearrange("p a b c d -> p (a b c d)")

        x0 = sb("x0", [P, G, D])
        xt0_s = sb("xt0_s", [P, DC, G, P])
        xt0_h = sb("xt0_h", [P, DC, G, P], F32R)
        xt0_l = sb("xt0_l", [P, DC, G, P], F32R)
        proj0 = sb("proj0", [P, G, D + 2])
        x1 = sb("x1", [P, G, D])
        att0 = Attention("att0", SLOPE_L0, bank_a0, bank_a1, proj0, D)
        norm0 = Norm("norm0")
        xt1_s = sb("xt1_s", [P, DC, G, P])
        proj1 = sb("proj1", [P, G, F1 + 2])
        x2 = sb("x2", [P, G, D])
        x2_h = sb("x2_h", [P, G, D], F32R)
        x2_l = sb("x2_l", [P, G, D], F32R)
        x2_b = sb("x2_b", [P, G, D])
        conv_h = sb("conv_h", [P, G, DC, 2, P], F32R)
        conv_l = sb("conv_l", [P, G, DC, 2, P], F32R)
        att1 = Attention("att1", SLOPE_L1, bank_b0, bank_b1, proj1, F1)
        norm1, norm2 = Norm("norm1"), Norm("norm2")
        x3 = sb("x3", [P, G, D])
        xt3_h = sb("xt3_h", [P, DC, G, P], F32R)
        xt3_l = sb("xt3_l", [P, DC, G, P], F32R)
        proj3 = sb("proj3", [P, G, HCOLS])
        top3 = sb("top3", [P, G, H])
        neg3 = sb("neg3", [P, G, H])
        neg_max3 = sb("neg_max3", [P, G, H])
        bias3 = sb("bias3", [P, G, 2, H])
        tick3 = sb("tick3", [P, 1])
        z3 = sb("z3", [P, G, H, P])
        e3 = sb("e3", [P, G, 2, H, P])
        p3 = sb("p3", [P, G, H, P])
        sum3 = sb("sum3", [P, G, H])
        rsum3 = sb("rsum3", [P, G, H])
        p3_t = sb("p3_t", [P, G, H, P])
        elu3 = sb("elu3", [P, 2, 512])
        h_s = sb("h_s", [P, H, DC, G, P])
        h_h = sb("h_h", [P, H, DC, G, P], F32R)
        h_l = sb("h_l", [P, H, DC, G, P], F32R)
        proj4 = sb("proj4", [P, G, D + 2])
        att4 = Attention("att4", SLOPE_L3, bank_d0, bank_d1, proj4, D)
        elu4 = sb("elu4", [P, 512])
        o_s = sb("o_s", [P, DC, G * P])
        o_h = sb("o_h", [P, DC, G * P], F32R)
        o_l = sb("o_l", [P, DC, G * P], F32R)
        relu_s = sb("relu_s", [P, DC, G * P])
        relu_h = sb("relu_h", [P, DC, G * P], F32R)
        relu_l = sb("relu_l", [P, DC, G * P], F32R)
        x3_b = sb("x3_b", [P, 2 * G, D])
        norm3, norm4 = Norm("norm3", on_act=True), Norm("norm4", on_act=True)
        n3 = sb("n3", [P, G, D])
        n3_g = sb("n3_g", [P, G, D])
        result = sb("result", [P, G, D])
        wh_s = flat(e3).rearrange("p (c f) -> p c f", c=DC)
        wo_s = flat(h_s).rearrange("p (c f) -> p c f", c=HC)
        w2_s = flat(p3).rearrange("p (k c f) -> p k c f", k=2, c=DC)
        ff_s = flat(p3_t).rearrange("p (k c f) -> p k c f", k=2, c=DC)
        ah_bc = flat(proj3)[:, 0:2 * H * D].rearrange("p (h k f) -> p h k f", h=H, k=2)
        ao_bc = flat(elu3)[:, 0:2 * D].rearrange("p (k f) -> p k f", k=2)
        junk = elu4[:, :].rearrange("p (k f) -> p k f", k=2)
        a0_bc = flat(o_s).rearrange("p (k f) -> p k f", k=2)
        a1_bc = flat(relu_s)[:, 0:2 * F1].rearrange("p (k f) -> p k f", k=2)
        b2_bc = flat(n3)[:, 0:D]

        made = sem("made")
        adj_in, adj_t_in = sem("adj_in"), sem("adj_t_in")
        a0_in, a1_in, ah_in, ao_in = (sem(f"a{k}_in") for k in "01ho")
        b2_in = sem("b2_in")
        vec_in = sem("vec_in")
        w0_in, w1_in, w2_in = sem("w0_in"), sem("w1_in"), sem("w2_in")
        wh_in, wo_in, ff_in = sem("wh_in"), sem("wo_in"), sem("ff_in")
        adj_made = sem("adj_made")
        attended = sem("attended")
        weights_hi = sem("weights_hi")
        w0_lo = sem("w0_lo")
        weights_lo = sem("weights_lo")
        x0_in, xt0_in = sem("x0_in"), sem("xt0_in")
        stored = sem("stored")
        xt1, xt3 = sem("xt1"), sem("xt3")
        hi0, hi3 = sem("hi0"), sem("hi3")
        lo0, lo3 = sem("lo0"), sem("lo3")
        xt1_kept = sem("xt1_kept")
        projected0 = sem("projected0")
        projected1 = sem("projected1")
        proj0_kept, proj1_kept = sem("proj0_kept"), sem("proj1_kept")
        gated0 = sem("gated0")
        mixed0, mixed1 = sem("mixed0"), sem("mixed1")
        summed1b = sem("summed1b")
        x2_hi, x2_lo, x2_biased = sem("x2_hi"), sem("x2_lo"), sem("x2_biased")
        conv = sem("conv")
        conv_hi, conv_lo = sem("conv_hi"), sem("conv_lo")
        conv_out = sem("conv_out")
        x3_biased = sem("x3_biased")
        head_proj, head_proj_kept = sem("head_proj"), sem("head_proj_kept")
        scored3 = sem("scored3")
        maxing3 = sem("maxing3")
        biased3, expd3 = sem("biased3"), sem("expd3")
        weighed3, inverted3 = sem("weighed3"), sem("inverted3")
        normal3 = sem("normal3")
        turned3, kept3 = sem("turned3"), sem("kept3")
        mixed3 = sem("mixed3")
        elu_exp3, elu_low3 = sem("elu_exp3"), sem("elu_low3")
        h_made, h_hi, h_lo = sem("h_made"), sem("h_hi"), sem("h_lo")
        projected4, proj4_kept = sem("projected4"), sem("proj4_kept")
        normal4 = sem("normal4")
        mixed4, elu_exp4, elu_low4 = sem("mixed4"), sem("elu_exp4"), sem("elu_low4")
        o_made, o_hi, o_lo = sem("o_made"), sem("o_hi"), sem("o_lo")
        ff1_out, ff2_out = sem("ff1_out"), sem("ff2_out")
        relu_made, relu_hi, relu_lo = sem("relu_made"), sem("relu_hi"), sem("relu_lo")
        scaled3 = sem("scaled3")
        block = ctx.enter_context(nc.Block())

        def over_rows(v):
            return v.rearrange("(a n) -> a n", a=1).to_broadcast([P, v.shape[0]])

        @block.sync
        def _(sp):
            def unit(src, n):
                return src[bass.ds(n * G, G), :, :].rearrange("b n d -> n b d")

            def load_xt(n):
                for b in range(G):
                    sp.dma_start(xt0_s[:, :, b, :], x_t[bass.ds(n * G + b, 1), :, :].rearrange(
                        "b (c p) n -> p (b c) n", p=P)).then_inc(xt0_in, 16)

            def load_x(n):
                sp.dma_start(x0[:, :, :], unit(x, n)).then_inc(x0_in, 16)

            sp.dma_start(w0_s[:, :, 0:D], w0.rearrange("(c p) f -> p c f", p=P)).then_inc(w0_in, 16)
            sp.dma_start(adj_i[:, :], adj[:, :]).then_inc(adj_in, 16)
            load_xt(0)
            sp.dma_start(adj_ti[:, :], adj_t[:, :]).then_inc(adj_t_in, 16)
            sp.dma_start(w1_s[:, :, 0:F1], w1.rearrange("(c p) f -> p c f", p=P)).then_inc(w1_in, 16)
            load_x(0)
            sp.dma_start(ah_bc.rearrange("p h k f -> p (h k f)"), over_rows(ah.rearrange("h f -> (h f)")))\
                .then_inc(ah_in, 16)
            sp.dma_start(w2_s, w2_t.rearrange("(k c p) f -> p k c f", k=2, p=P)).then_inc(w2_in, 16)
            for h in range(H):
                sp.dma_start(wh_s[:, :, h * D:(h + 1) * D],
                             wh[h, :, :].rearrange("(c p) f -> p c f", p=P)).then_inc(wh_in, 16)

            def load_next_xt(s):
                if s.last:
                    return
                sp.wait_ge(lo0, s.n)
                load_xt(s.n)

            def load_rest(s):
                if s.again:
                    return
                sp.dma_start(ff_s[:, 0, :, :], ff1.rearrange("(c p) f -> p c f", p=P)).then_inc(ff_in, 16)
                sp.dma_start(ff_s[:, 1, :, :], ff2.rearrange("(c p) f -> p c f", p=P)).then_inc(ff_in, 16)
                sp.dma_start(ao_bc.rearrange("p k f -> p (k f)"), over_rows(ao)).then_inc(ao_in, 16)
                sp.dma_start(wo_s, wo.rearrange("(c p) f -> p c f", p=P)).then_inc(wo_in, 16)

                sp.dma_start(fb1_c[:, :], fb1_t[:, :]).then_inc(vec_in, 16)
                for dst, src in ((fb2_bc[:, :], fb2), (gamma_bc[:, :], gamma), (beta_bc[:, :], beta)):
                    sp.dma_start(dst, over_rows(src)).then_inc(vec_in, 16)

            def load_next(s):
                if s.last:
                    return
                sp.wait_ge(norm0.summed, s.n)
                load_x(s.n)

            def store(s):
                sp.wait_ge(norm4.done, s.n)
                sp.dma_start(unit(out, s.before), result[:, :, :]).then_inc(stored, 16)

            def turn(u):
                u.at(0, load_next_xt)
                u.at(0, load_rest)
                u.at(2, load_next)
                u.at(7, store)

            run_turns(sp, turn)
            sp.wait_ge(stored, 16 * UNITS)

        @block.gpsimd
        def _(pool):
            def variance_eps(s, norm):
                pool.wait_ge(norm.averaged, s.n * 2)
                if norm.on_act:
                    if s.again:
                        pool.wait_ge(norm.done, s.before)
                    pool.tensor_tensor(norm.shift[:, 0, :], zero_c[:, :], norm.moments[:, :, 0], ALU.subtract)
                pool.tensor_tensor(norm.var_eps[:, :], norm.moments[:, :, 1], eps_c[:, :], ALU.add)\
                    .then_inc(norm.scaled, 1)

            def rstd(s, norm):
                pool.wait_ge(norm.scaled, s.n * norm.raises - (norm.raises - 1))
                pool.tensor_tensor(norm.rstd[:, :], norm.var_eps[:, :], half_c[:, :], ALU.pow)\
                    .then_inc(norm.scaled, 1)

            def shift(s, norm):
                pool.wait_ge(norm.scaled, s.n * 3 - 1)
                pool.tensor_tensor(norm.shift[:, 1, :], norm.shift[:, 0, :], norm.rstd[:, :], ALU.mult)\
                    .then_inc(norm.scaled, 1)

            def a_low(s):
                pool.wait_ge(hi0, s.n)
                if s.again:
                    pool.wait_ge(projected0, s.before * G)
                pool.tensor_tensor(flat(xt0_l), flat(xt0_s), flat(xt0_h).bitcast(F32), ALU.subtract)\
                    .then_inc(lo0, 1)

            def b_second_half(s):
                pool.wait_ge(proj1_kept, s.n)
                if s.again:
                    pool.wait_ge(norm1.done, s.before)
                pool.tensor_tensor(norm1.y[:, :, F1:D], proj1[:, :, 0:F1], x1[:, :, F1:D], ALU.add)\
                    .then_inc(summed1b, 1)

            def b_low(s):
                pool.wait_ge(x2_hi, s.n)
                pool.tensor_tensor(x2_l[:, :, :], x2[:, :, :], x2_h[:, :, :].bitcast(F32), ALU.subtract)\
                    .then_inc(x2_lo, 1)

            def b_bias(s):
                if not s.again:
                    pool.wait_ge(adj_made, ADJ_MADE)
                pool.wait_ge(norm1.done, s.n)
                if s.again:
                    pool.wait_ge(norm2.summed, s.before)
                pool.tensor_tensor(x2_b[:, :, :], x2[:, :, :],
                                   deg_b[:, :].unsqueeze(1).to_broadcast([P, G, D]), ALU.add)\
                    .then_inc(x2_biased, 1)

            def c_bias(s):
                pool.wait_ge(norm2.done, s.n)
                if s.third:
                    pool.wait_ge(norm4.summed, s.two_before)
                if s.again:
                    pool.wait_ge(x3_biased, s.before)
                pool.tensor_tensor(tick[:, :], zero_c[:, :], eps_c[:, :], ALU.add)
                pool.tensor_tensor(x3_b[:, bass.ds(s.before % 2 * G, G), :], x3[:, :, :],
                                   beta_bc[:, :].unsqueeze(1).to_broadcast([P, G, D]), ALU.add)\
                    .then_inc(x3_biased, 1)

            def c_normalise(s, b):
                pool.wait_ge(inverted3, s.n * G - (G - 1 - b))
                pool.tensor_tensor(p3[:, b, :, :], p3[:, b, :, :],
                                   rsum3[:, b, :].unsqueeze(2).to_broadcast([P, H, P]), ALU.mult)\
                    .then_inc(normal3, 1)

            def c_head_low(s, h):
                pool.wait_ge(h_hi, s.n * H - (H - 1 - h))
                pool.tensor_tensor(h_l[:, h, :, :, :], h_s[:, h, :, :, :], h_h[:, h, :, :, :].bitcast(F32),
                                   ALU.subtract).then_inc(h_lo, 1)

            def d_normalise(s):
                pool.wait_ge(att4.inverted, s.n)
                pool.tensor_tensor(att4.p[:, :, :], att4.p[:, :, :],
                                   att4.rsum[:, :].unsqueeze(2).to_broadcast([P, G, P]), ALU.mult)\
                    .then_inc(normal4, 1)

            def d_output_low(s):
                pool.wait_ge(o_hi, s.n)
                pool.tensor_tensor(o_l[:, :, :], o_s[:, :, :], o_h[:, :, :].bitcast(F32), ALU.subtract)\
                    .then_inc(o_lo, 1)

            def d_relu_low(s):
                pool.wait_ge(relu_hi, s.n)
                pool.tensor_tensor(relu_l[:, :, :], relu_s[:, :, :], relu_h[:, :, :].bitcast(F32), ALU.subtract)\
                    .then_inc(relu_lo, 1)

            def d_gamma(s):
                pool.wait_ge(norm3.done, s.n)
                if s.again:
                    pool.wait_ge(norm4.summed, s.before)
                pool.tensor_tensor(n3_g[:, :, :], n3[:, :, :],
                                   gamma_bc[:, :].unsqueeze(1).to_broadcast([P, G, D]), ALU.mult)\
                    .then_inc(scaled3, 1)

            def low(dst, src, hi, in_order):
                pool.wait_ge(weights_hi, in_order)
                return pool.tensor_tensor(dst, src, hi.bitcast(F32), ALU.subtract)

            def low_l2(s):
                if s.again:
                    return
                low(w2_l[:, :, :, :], w2_s, w2_h[:, :, :, :], W2_HI).then_inc(weights_lo, 1)

            def low_heads(s):
                if s.again:
                    return
                low(wh_l[:, :, 2 * H:HCOLS], wh_s, wh_h[:, :, 2 * H:HCOLS], WH_HI)

            def low_head_columns(s):
                if s.again:
                    return
                low(wh_l[:, :, 0:2 * H], wha_s[:, :, :], wh_h[:, :, 0:2 * H], WHA_HI).then_inc(weights_lo, 1)

            def low_ff(s):
                if s.again:
                    return
                low(ff1_l[:, :, :], ff_s[:, 0, :, :], ff1_h[:, :, :], FF_HI)
                low(ff2_l[:, :, :], ff_s[:, 1, :, :], ff2_h[:, :, :], FF_HI).then_inc(weights_lo, 1)

            def low_out(s):
                if s.again:
                    return
                low(wo_l[:, :, 0:D], wo_s, wo_h[:, :, 0:D], WO_HI)

            def low_out_columns(s):
                if s.again:
                    return
                low(wo_l[:, :, D:D + 2], woa_s[:, :, :], wo_h[:, :, D:D + 2], WOA_HI).then_inc(weights_lo, 1)
                pool.wait_ge(vec_in, 16 * VECTORS)

            def turn(u):
                u.at(6, d_normalise)
                u.at(5, c_normalise, 1)
                u.at(4, variance_eps, norm2)
                u.at(4, rstd, norm2)
                u.at(7, variance_eps, norm4)
                u.at(7, rstd, norm4)
                u.at(6, d_output_low)
                u.at(3, b_second_half)
                u.at(5, c_head_low, 0)
                u.at(7, shift, norm4)
                u.at(6, d_relu_low)
                u.at(5, c_head_low, 1)
                u.at(5, c_head_low, 2)
                u.at(5, c_head_low, 3)
                u.at(6, variance_eps, norm3)
                u.at(6, rstd, norm3)
                u.at(6, shift, norm3)
                u.at(3, variance_eps, norm1)
                u.at(3, rstd, norm1)
                u.at(2, variance_eps, norm0)
                u.at(6, d_gamma)
                u.at(2, rstd, norm0)
                u.at(2, low_l2)
                u.at(2, low_heads)
                u.at(3, b_low)
                u.at(4, c_normalise, 0)
                u.at(3, b_bias)
                u.at(3, low_ff)
                u.at(3, low_head_columns)
                u.at(3, low_out)
                u.at(4, c_bias)
                u.at(4, low_out_columns)
                u.at(0, a_low)

            pool.memset(ident[:, :], 0.0).then_inc(made, 1)
            pool.memset(eps_c[:, :], EPS).then_inc(made, 1)
            pool.memset(zero_c[:, :], 0.0).then_inc(made, 1)
            pool.memset(half_c[:, :], -0.5).then_inc(made, 1)
            pool.wait_ge(made, 4)
            pool.affine_select(out=ident[:, :], in_=ident[:, :], compare_op=ALU.not_equal, fill=1.0, base=0,
                               pattern=[[-1, P]], channel_multiplier=1).then_inc(made, 1)
            run_turns(pool, turn)

        @block.tensor
        def _(pe):
            def transpose_x(src, dst):
                for c in range(DC):
                    for b in range(G):
                        k = c * G + b
                        last = nc.tensor.transpose(dst[:, k * P:(k + 1) * P], src[:, b, c * P:(c + 1) * P],
                                                   ident[:, :])
                return last

            def product(dst, pairs, open_end=False):
                for k, (left, right) in enumerate(pairs):
                    last = nc.tensor.matmul(dst, left, right, start=(k == 0),
                                            stop=(k == len(pairs) - 1 and not open_end))
                return last

            def parts(left_h, left_l, right_h, right_l, chunks):
                return [(left(c), right(c)) for left, right in ((left_l, right_h), (left_h, right_l),
                                                                (left_h, right_h)) for c in chunks]

            def scores(s, att):
                for b in range(G):
                    last = nc.tensor.transpose(att.scores[:, b * P:(b + 1) * P],
                                               att.d[:, b, :].to_broadcast([P, P]), ident[:, :])
                last.then_inc(att.scored, 1)

            def turn_weights(s, att):
                for b in range(G):
                    last = nc.tensor.transpose(att.probs[:, b * P:(b + 1) * P], att.p[:, b, :], ident[:, :])
                last.then_inc(att.turned, 1)

            def a_project(s):
                if not s.again:
                    pe.wait_ge(w0_lo, 1)
                pe.wait_ge(lo0, s.n)
                if s.again:
                    pe.wait_ge(norm0.summed, s.before)
                for b, dst in enumerate((bank_a0, bank_a1)):
                    product(dst[:, 0:D + 2], parts(lambda c: xt0_h[:, c, b, :], lambda c: xt0_l[:, c, b, :],
                                                   lambda c: w0_h[:, c, :], lambda c: w0_l[:, c, :], range(DC)))\
                        .then_inc(projected0, 1)

            def a_scores(s):
                pe.wait_ge(proj0_kept, s.n)
                scores(s, att0)

            def a_turn(s):
                pe.wait_ge(att0.weighed, s.n)
                turn_weights(s, att0)

            def a_mix(s):
                pe.wait_ge(att0.kept, s.n)
                for b in range(G):
                    last = product(bank_a0[:, b * D:(b + 1) * D], [(att0.p_t[:, b, :], proj0[:, b, 0:D])])
                last.then_inc(mixed0, 1)

            def b_transpose(s):
                pe.wait_ge(norm0.done, s.n)
                if s.again:
                    pe.wait_ge(conv_lo, s.before * G)
                transpose_x(x1, bank_b0).then_inc(xt1, 1)

            def b_project(s):
                if not s.again:
                    pe.wait_ge(attended, W1_COLUMNS)
                    pe.wait_ge(w1_in, 16)
                pe.wait_ge(xt1_kept, s.n)
                if s.again:
                    pe.wait_ge(norm2.summed, s.before)
                for b in range(G):
                    last = product(bank_b1[:, b * (F1 + 2):(b + 1) * (F1 + 2)],
                                   [(xt1_s[:, c, b, :], w1_s[:, c, :]) for c in range(DC)])
                last.then_inc(projected1, 1)

            def b_scores(s):
                pe.wait_ge(proj1_kept, s.n)
                scores(s, att1)

            def b_turn(s):
                pe.wait_ge(att1.weighed, s.n)
                turn_weights(s, att1)

            def b_mix(s):
                pe.wait_ge(att1.kept, s.n)
                for b in range(G):
                    last = product(bank_b0[:, b * F1:(b + 1) * F1], [(att1.p_t[:, b, :], proj1[:, b, 0:F1])])
                last.then_inc(mixed1, 1)

            def b_convolve(s, b):
                if not s.again and b == 0:
                    pe.wait_ge(adj_made, ADJ_DEG)
                if b == 0:
                    pe.wait_ge(x2_lo, s.n)
                else:
                    pe.wait_ge(norm1.summed, s.n)
                for c in range(DC):
                    last = product((bank_b1, bank_b0)[b][:, c * 2 * P:(c + 1) * 2 * P],
                                   [(part[:, b, c * P:(c + 1) * P], adj_deg[:, :, :]) for part in (x2_l, x2_h)])
                last.then_inc(conv, 1)

            def b_conv_project(s, b):
                if not s.again and b == 0:
                    pe.wait_ge(weights_lo, W2_LO)
                pe.wait_ge(conv_lo, s.n * G - (G - 1 - b))
                last = product(bank_b1[:, b * D:(b + 1) * D],
                               parts(lambda k: conv_h[:, b, k[0], k[1], :], lambda k: conv_l[:, b, k[0], k[1], :],
                                     lambda k: w2_h[:, 1 - k[1], k[0], :], lambda k: w2_l[:, 1 - k[1], k[0], :],
                                     [(c, k) for c in range(DC) for k in range(2)]))
                if b == G - 1:
                    last.then_inc(conv_out, 1)

            def c_transpose(s):
                pe.wait_ge(norm2.done, s.n)
                if s.again:
                    pe.wait_ge(h_made, s.before * H - 1)
                transpose_x(x3, bank_c0).then_inc(xt3, 1)

            def c_project(s, k):
                if not s.again and k == 0:
                    pe.wait_ge(weights_lo, WH_LO)
                if k == 0:
                    pe.wait_ge(lo3, s.n)
                    if s.again:
                        pe.wait_ge(h_made, s.before * H)
                else:
                    pe.wait_ge(head_proj_kept, s.n * FILLS - (FILLS - k))
                b, third = FILL_ORDER[k]
                cols = slice(third * FILL, (third + 1) * FILL)
                product(bank_c1[:, 0:FILL],
                        parts(lambda c: xt3_h[:, c, b, :], lambda c: xt3_l[:, c, b, :],
                              lambda c: wh_h[:, c, cols], lambda c: wh_l[:, c, cols], range(DC)))\
                    .then_inc(head_proj, 1)

            def c_scores(s, b):
                pe.wait_ge(head_proj_kept, s.n * FILLS - (FILLS - 1 - b))
                if b:
                    pe.wait_ge(maxing3, s.n * 6 - 5)
                for h in range(H):
                    last = nc.tensor.transpose(bank_c0[:, h * P:(h + 1) * P],
                                               proj3[:, b, H + h:H + h + 1].to_broadcast([P, P]), ident[:, :])
                last.then_inc(scored3, 1)

            def c_turn(s, b):
                if not s.again and b == 0:
                    pe.wait_ge(weights_lo, FF_LO)
                pe.wait_ge(normal3, s.n * G - (G - 1 - b))
                if b == 0:
                    pe.wait_ge(maxing3, s.n * 6 - 2)
                else:
                    pe.wait_ge(head_proj_kept, s.n * FILLS)
                for h in range(H):
                    last = nc.tensor.transpose((bank_c0, bank_c1)[b][:, h * P:(h + 1) * P], p3[:, b, h, :],
                                               ident[:, :])
                last.then_inc(turned3, 1)

            def c_mix(s, h):
                if not s.again and h == 0:
                    pe.wait_ge(weights_lo, WO_LO)
                if h < 2:
                    pe.wait_ge(kept3, s.n * G)
                else:
                    pe.wait_ge(h_made, s.n * H - (H + 1 - h))
                for c in range(DC):
                    for b in range(G):
                        k, f = c * G + b, 2 * H + h * D + c * P
                        last = product((bank_c0, bank_c1)[h % 2][:, k * P:(k + 1) * P],
                                       [(proj3[:, b, f:f + P], p3_t[:, b, h, :])])
                last.then_inc(mixed3, 1)

            def d_project(s, b):
                if b == 0:
                    pe.wait_ge(h_lo, s.n * H)
                    if s.again:
                        pe.wait_ge(o_made, s.before)
                elif s.again:
                    pe.wait_ge(norm3.summed, s.before)
                product((bank_d0, bank_d1)[b][:, 0:D + 2],
                        parts(lambda k: h_h[:, k // DC, k % DC, b, :], lambda k: h_l[:, k // DC, k % DC, b, :],
                              lambda k: wo_h[:, k, :], lambda k: wo_l[:, k, :], range(HC)))\
                    .then_inc(projected4, 1)

            def d_scores(s):
                pe.wait_ge(proj4_kept, s.n * G)
                scores(s, att4)

            def d_turn(s):
                pe.wait_ge(normal4, s.n)
                turn_weights(s, att4)

            def d_mix(s):
                pe.wait_ge(att4.kept, s.n)
                for c in range(DC):
                    for b in range(G):
                        k = c * G + b
                        last = product(bank_d0[:, k * P:(k + 1) * P],
                                       [(proj4[:, b, c * P:(c + 1) * P], att4.p_t[:, b, :])])
                last.then_inc(mixed4, 1)

            def d_ff1(s):
                pe.wait_ge(o_lo, s.n)
                for m in range(DC):
                    cols = slice(m * P, (m + 1) * P)
                    last = product(bank_d1[:, m * G * P:(m + 1) * G * P],
                                   parts(lambda c: ff1_h[:, c, cols], lambda c: ff1_l[:, c, cols],
                                         lambda c: o_h[:, c, :], lambda c: o_l[:, c, :], range(DC)))
                last.then_inc(ff1_out, 1)

            def d_ff2(s):
                pe.wait_ge(relu_lo, s.n)
                for b in range(G):
                    rows = slice(b * P, (b + 1) * P)
                    product(bank_d1[:, b * D:(b + 1) * D],
                            parts(lambda c: relu_h[:, c, rows], lambda c: relu_l[:, c, rows],
                                  lambda c: ff2_h[:, c, :], lambda c: ff2_l[:, c, :], range(DC)), open_end=True)
                    for c in range(DC):
                        last = nc.tensor.matmul(bank_d1[:, b * D + c * P:b * D + (c + 1) * P], o_s[:, c, rows],
                                                ident[:, :], is_transpose=True, start=False, stop=(c == DC - 1))
                last.then_inc(ff2_out, 1)

            def turn(u):
                u.at(5, c_project, 4)
                u.at(4, b_conv_project, 1)
                u.at(3, b_transpose)
                u.at(6, d_turn)
                u.at(5, c_project, 5)
                u.at(6, d_mix)
                u.at(2, a_turn)
                u.at(5, c_turn, 1)
                u.at(3, b_project)
                u.at(5, c_mix, 0)
                u.at(3, b_scores)
                u.at(5, c_mix, 1)
                u.at(2, a_mix)
                u.at(6, d_ff1)
                u.at(5, c_mix, 2)
                u.at(3, b_turn)
                u.at(5, c_mix, 3)
                u.at(1, a_project)
                u.at(4, c_transpose)
                u.at(6, d_ff2)
                u.at(4, c_project, 0)
                u.at(3, b_mix)
                u.at(1, a_scores)
                u.at(4, c_scores, 0)
                u.at(4, c_project, 1)
                u.at(5, d_project, 0)
                u.at(4, c_scores, 1)
                u.at(5, d_project, 1)
                u.at(4, c_project, 2)
                u.at(3, b_convolve, 0)
                u.at(5, d_scores)
                u.at(3, b_convolve, 1)
                u.at(4, c_project, 3)
                u.at(4, c_turn, 0)
                u.at(3, b_conv_project, 0)

            pe.wait_ge(made, 5)
            run_turns(pe, turn)

        @block.scalar
        def _(act):
            def exps(s, att):
                act.wait_ge(att.biased, s.n)
                for b in range(G):
                    z = att.scores[:, b * P:(b + 1) * P]
                    nc.scalar.activation(att.e1[:, b, :], z, ACT.Exp, bias=att.bias[:, 0, b:b + 1])
                    last = nc.scalar.activation(att.e2[:, b, :], z, ACT.Exp, bias=att.bias[:, 1, b:b + 1],
                                                scale=att.slope)
                last.then_inc(att.expd, 1)

            def keep_weights(s, att):
                act.wait_ge(att.turned, s.n)
                nc.scalar.copy(flat(att.p_t), att.probs[:, 0:G * P]).then_inc(att.kept, 1)

            def norm_apply(s, norm, dst):
                act.wait_ge(norm.scaled, s.n * 3)
                for b in range(G):
                    last = nc.scalar.activation(dst[:, b, :], norm.y[:, b, :], ACT.Identity,
                                                bias=norm.shift[:, 1, b:b + 1], scale=norm.rstd[:, b:b + 1])
                last.then_inc(norm.done, 1)

            def a_high(s):
                act.wait_ge(xt0_in, s.n * 32)
                if s.again:
                    act.wait_ge(projected0, s.before * G)
                nc.scalar.copy(flat(xt0_h), flat(xt0_s)).then_inc(hi0, 1)

            def a_keep(s):
                if s.again:
                    act.wait_ge(mixed0, s.before)
                for b, src in enumerate((bank_a0, bank_a1)):
                    act.wait_ge(projected0, s.n * G - (G - 1 - b))
                    last = nc.scalar.copy(proj0[:, b, :], src[:, 0:D + 2])
                last.then_inc(proj0_kept, 1)

            def b_keep_x(s):
                act.wait_ge(xt1, s.n)
                if s.again:
                    act.wait_ge(projected1, s.before)
                nc.scalar.copy(flat(xt1_s), bank_b0[:, :]).then_inc(xt1_kept, 1)

            def b_keep(s):
                act.wait_ge(projected1, s.n)
                if s.again:
                    act.wait_ge(mixed1, s.before)
                    act.wait_ge(summed1b, s.before)
                nc.scalar.copy(flat(proj1), bank_b1[:, 0:G * (F1 + 2)]).then_inc(proj1_kept, 1)

            def b_high(s):
                act.wait_ge(norm1.done, s.n)
                if s.again:
                    act.wait_ge(conv, s.before * G)
                nc.scalar.copy(x2_h[:, :, :], x2[:, :, :]).then_inc(x2_hi, 1)

            def b_conv_high(s, b):
                act.wait_ge(conv, s.n * G - (G - 1 - b))
                if s.again and b == 0:
                    act.wait_ge(conv_out, s.before)
                nc.scalar.copy(conv_h[:, b, :, :, :].rearrange("p c k n -> p (c k n)"),
                               (bank_b1, bank_b0)[b][:, :]).then_inc(conv_hi, 1)

            def c_high(s):
                act.wait_ge(xt3, s.n)
                if s.again:
                    act.wait_ge(head_proj, s.before * FILLS)
                nc.scalar.copy(flat(xt3_h), bank_c0[:, :]).then_inc(hi3, 1)

            def c_keep(s, k):
                act.wait_ge(head_proj, s.n * FILLS - (FILLS - 1 - k))
                if s.again and k == 0:
                    act.wait_ge(mixed3, s.before * H)
                b, third = FILL_ORDER[k]
                nc.scalar.copy(proj3[:, b, third * FILL:(third + 1) * FILL],
                               bank_c1[:, 0:FILL]).then_inc(head_proj_kept, 1)

            def c_exps(s, b):
                act.wait_ge(biased3, s.n * G - (G - 1 - b))
                for h in range(H):
                    nc.scalar.activation(e3[:, b, 0, h, :], z3[:, b, h, :], ACT.Exp, bias=bias3[:, b, 0, h:h + 1])
                    last = nc.scalar.activation(e3[:, b, 1, h, :], z3[:, b, h, :], ACT.Exp,
                                                bias=bias3[:, b, 1, h:h + 1], scale=SLOPE_L3)
                last.then_inc(expd3, 1)

            def c_keep_weights(s, b):
                act.wait_ge(turned3, s.n * G - (G - 1 - b))
                nc.scalar.copy(p3_t[:, b, :, :].rearrange("p h n -> p (h n)"), (bank_c0, bank_c1)[b][:, :])\
                    .then_inc(kept3, 1)

            def c_elu_exp(s, h):
                act.wait_ge(mixed3, s.n * H - (H - 1 - h))
                nc.scalar.activation(elu3[:, h % 2, :], (bank_c0, bank_c1)[h % 2][:, :], ACT.Exp)\
                    .then_inc(elu_exp3, 1)

            def c_head_high(s, h):
                act.wait_ge(h_made, s.n * H - (H - 1 - h))
                if s.again and h == 0:
                    act.wait_ge(projected4, s.before * G)
                nc.scalar.copy(h_h[:, h, :, :, :], h_s[:, h, :, :, :]).then_inc(h_hi, 1)

            def d_keep(s, b):
                act.wait_ge(projected4, s.n * G - (G - 1 - b))
                if s.again and b == 0:
                    act.wait_ge(mixed4, s.before)
                nc.scalar.copy(proj4[:, b, :], (bank_d0, bank_d1)[b][:, 0:D + 2]).then_inc(proj4_kept, 1)

            def d_elu_exp(s):
                act.wait_ge(mixed4, s.n)
                nc.scalar.activation(elu4[:, :], bank_d0[:, :], ACT.Exp).then_inc(elu_exp4, 1)

            def d_output_high(s):
                act.wait_ge(o_made, s.n)
                nc.scalar.copy(o_h[:, :, :], o_s[:, :, :]).then_inc(o_hi, 1)

            def d_relu(s):
                act.wait_ge(ff1_out, s.n)
                for m in range(DC):
                    last = nc.scalar.activation(relu_s[:, m, :], bank_d1[:, m * G * P:(m + 1) * G * P],
                                                ACT.Relu, bias=fb1_c[:, m:m + 1])
                last.then_inc(relu_made, 1)

            def d_relu_high(s):
                act.wait_ge(relu_made, s.n)
                nc.scalar.copy(relu_h[:, :, :], relu_s[:, :, :]).then_inc(relu_hi, 1)

            def d_norm3(s):
                if s.again:
                    act.wait_ge(scaled3, s.before)
                norm_apply(s, norm3, n3)

            def d_norm4(s):
                if s.again:
                    act.wait_ge(stored, s.before * 16)
                norm_apply(s, norm4, result)

            def high_l0(s):
                if s.again:
                    return
                act.wait_ge(attended, W0_COLUMNS)
                act.wait_ge(w0_in, 16)
                nc.scalar.copy(w0_h[:, :, :], w0_s[:, :, :]).then_inc(weights_hi, 1)

            def high_l2(s):
                if s.again:
                    return
                act.wait_ge(w2_in, 16)
                nc.scalar.copy(w2_h[:, :, :, :], w2_s).then_inc(weights_hi, 1)

            def high_heads(s):
                if s.again:
                    return
                act.wait_ge(wh_in, 16 * H)
                nc.scalar.copy(wh_h[:, :, 2 * H:HCOLS], wh_s).then_inc(weights_hi, 1)

            def high_head_columns(s):
                if s.again:
                    return
                act.wait_ge(attended, WH_COLUMNS)
                nc.scalar.copy(wh_h[:, :, 0:2 * H], wha_s[:, :, :]).then_inc(weights_hi, 1)

            def high_ff_out(s):
                if s.again:
                    return
                act.wait_ge(ff_in, 32)
                nc.scalar.copy(ff1_h[:, :, :], ff_s[:, 0, :, :])
                nc.scalar.copy(ff2_h[:, :, :], ff_s[:, 1, :, :]).then_inc(weights_hi, 1)
                act.wait_ge(wo_in, 16)
                nc.scalar.copy(wo_h[:, :, 0:D], wo_s).then_inc(weights_hi, 1)

            def high_out_columns(s):
                if s.again:
                    return
                act.wait_ge(attended, WO_COLUMNS)
                nc.scalar.copy(wo_h[:, :, D:D + 2], woa_s[:, :, :]).then_inc(weights_hi, 1)
                act.wait_ge(vec_in, 16 * VECTORS)

            def turn(u):
                u.at(4, b_conv_high, 1)
                u.at(5, c_keep, 3)
                u.at(6, exps, att4)
                u.at(5, c_exps, 1)
                u.at(5, c_keep, 4)
                u.at(6, keep_weights, att4)
                u.at(3, b_keep_x)
                u.at(5, c_keep, 5)
                u.at(5, c_keep_weights, 0)
                u.at(6, d_elu_exp)
                u.at(5, c_keep_weights, 1)
                u.at(2, keep_weights, att0)
                u.at(2, high_heads)
                u.at(2, high_ff_out)
                u.at(3, b_keep)
                u.at(6, d_output_high)
                u.at(5, c_elu_exp, 0)
                u.at(5, c_elu_exp, 1)
                u.at(3, exps, att1)
                u.at(3, high_head_columns)
                u.at(5, c_head_high, 0)
                u.at(6, d_relu)
                u.at(5, c_elu_exp, 2)
                u.at(6, d_relu_high)
                u.at(5, c_elu_exp, 3)
                u.at(3, keep_weights, att1)
                u.at(5, c_head_high, 1)
                u.at(4, c_high)
                u.at(4, high_out_columns)
                u.at(5, c_head_high, 2)
                u.at(5, c_head_high, 3)
                u.at(1, a_keep)
                u.at(1, high_l2)
                u.at(4, c_keep, 0)
                u.at(7, d_norm4)
                u.at(4, c_keep, 1)
                u.at(6, d_norm3)
                u.at(4, c_exps, 0)
                u.at(3, b_high)
                u.at(5, d_keep, 0)
                u.at(1, exps, att0)
                u.at(5, d_keep, 1)
                u.at(4, c_keep, 2)
                u.at(3, b_conv_high, 0)
                u.at(0, a_high)
                u.at(0, high_l0)

            act.dma_start(a0_bc[:, 0, :], over_rows(a0_src)).then_inc(a0_in, 16)
            act.dma_start(a0_bc[:, 1, :], over_rows(a0_dst)).then_inc(a0_in, 16)
            act.dma_start(a1_bc.rearrange("p k f -> p (k f)"), over_rows(a1.rearrange("k f -> (k f)")))\
                .then_inc(a1_in, 16)
            act.dma_start(b2_bc, over_rows(b2)).then_inc(b2_in, 16)
            run_turns(act, turn)

        @block.vector
        def _(dve):
            def masked_max(z, d, top):
                return nc.vector.tensor_tensor_reduce(z, d, mask[:, :], 1.0, LOWEST, ALU.add, ALU.max, top)

            def top(s, att):
                dve.wait_ge(att.scored, s.n)
                nc.vector.tensor_copy(att.tick[:, :], eps_c[:, 0:1])
                for b in range(G):
                    z = att.scores[:, b * P:(b + 1) * P]
                    last = masked_max(z, z, att.top[:, b:b + 1])
                last.then_inc(att.maxing, 1)

            def s_of(att):
                return att.s.rearrange("p b k -> p (b k)")

            def neg(s, att):
                dve.wait_ge(att.maxing, s.n * 3 - 2)
                nc.vector.scalar_tensor_tensor(att.neg[:, :], s_of(att), -1.0, att.top[:, :],
                                               ALU.mult, ALU.subtract).then_inc(att.maxing, 1)

            def neg_max(s, att):
                dve.wait_ge(att.maxing, s.n * 3 - 1)
                nc.vector.scalar_tensor_tensor(att.neg_max[:, :], att.neg[:, :], att.slope, att.neg[:, :],
                                               ALU.mult, ALU.min).then_inc(att.maxing, 1)

            def biases(s, att):
                dve.wait_ge(att.maxing, s.n * 3)
                for k, factor in enumerate((1.0, att.slope)):
                    last = nc.vector.scalar_tensor_tensor(att.bias[:, k, :], s_of(att), factor,
                                                          att.neg_max[:, :], ALU.mult, ALU.add)
                last.then_inc(att.biased, 1)

            def weigh(s, att):
                dve.wait_ge(att.expd, s.n)
                for b in range(G):
                    last = nc.vector.scalar_tensor_tensor(att.p[:, b, :], att.e1[:, b, :], 1.0, att.e2[:, b, :],
                                                          ALU.mult, ALU.max, accum_out=att.sum[:, b:b + 1])
                last.then_inc(att.weighed, 1)

            def invert(s, att):
                dve.wait_ge(att.weighed, s.n)
                nc.vector.reciprocal(att.rsum[:, :], att.sum[:, :]).then_inc(att.inverted, 1)

            def statistics(s, norm):
                dve.wait_ge(norm.summed, s.n)
                for b in range(G):
                    last = nc.vector.bn_stats(norm.stats[:, b, :], norm.y[:, b, :])
                last.then_inc(norm.averaged, 1)

            def moments(s, norm):
                dve.wait_ge(norm.averaged, s.n * 2 - 1)
                nc.vector.tensor_copy(norm.tick[:, :], eps_c[:, 0:1])
                for b in range(G):
                    last = nc.vector.bn_aggr(norm.moments[:, b, :], norm.stats[:, b, :])
                last.then_inc(norm.averaged, 1)

            def norm_apply(s, norm, dst):
                dve.wait_ge(norm.scaled, s.n * 2)
                for b in range(G):
                    last = nc.vector.tensor_scalar(dst[:, b, :], norm.y[:, b, :], norm.moments[:, b, 0:1],
                                                   norm.rstd[:, b:b + 1], ALU.subtract, ALU.mult)
                last.then_inc(norm.done, 1)

            def a_gate(s):
                dve.wait_ge(att0.inverted, s.n)
                nc.vector.tensor_scalar(att0.rsum[:, :], att0.rsum[:, :], has_neighbour[:, 0:1], None, ALU.mult)\
                    .then_inc(gated0, 1)

            def a_sum(s):
                dve.wait_ge(x0_in, s.n * 16)
                dve.wait_ge(gated0, s.n)
                dve.wait_ge(mixed0, s.n)
                for b in range(G):
                    last = nc.vector.scalar_tensor_tensor(norm0.y[:, b, :], bank_a0[:, b * D:(b + 1) * D],
                                                          att0.rsum[:, b:b + 1], x0[:, b, :], ALU.mult, ALU.add)
                last.then_inc(norm0.summed, 1)

            def a_norm(s):
                if s.again:
                    dve.wait_ge(summed1b, s.before)
                    dve.wait_ge(norm1.summed, s.before)
                norm_apply(s, norm0, x1)

            def b_sum(s):
                dve.wait_ge(att1.inverted, s.n)
                dve.wait_ge(mixed1, s.n)
                for b in range(G):
                    last = nc.vector.scalar_tensor_tensor(norm1.y[:, b, 0:F1], bank_b0[:, b * F1:(b + 1) * F1],
                                                          att1.rsum[:, b:b + 1], x1[:, b, 0:F1], ALU.mult, ALU.add)
                last.then_inc(norm1.summed, 1)

            def b_statistics(s):
                dve.wait_ge(summed1b, s.n)
                statistics(s, norm1)

            def b_norm1(s):
                if s.again:
                    dve.wait_ge(x2_lo, s.before)
                    dve.wait_ge(x2_biased, s.before)
                norm_apply(s, norm1, x2)

            def b_conv_low(s, b):
                dve.wait_ge(conv_hi, s.n * G - (G - 1 - b))
                nc.vector.tensor_tensor(conv_l[:, b, :, :, :].rearrange("p c k n -> p (c k n)"),
                                        (bank_b1, bank_b0)[b][:, :],
                                        conv_h[:, b, :, :, :].rearrange("p c k n -> p (c k n)").bitcast(F32),
                                        ALU.subtract).then_inc(conv_lo, 1)

            def b_conv_sum(s):
                dve.wait_ge(x2_biased, s.n)
                dve.wait_ge(conv_out, s.n)
                nc.vector.tensor_tensor(norm2.y[:, :, :], bank_b1[:, :].rearrange("p (b f) -> p b f", b=G),
                                        x2_b[:, :, :], ALU.add).then_inc(norm2.summed, 1)

            def b_norm2(s):
                if s.again:
                    dve.wait_ge(x3_biased, s.before)
                    dve.wait_ge(xt3, s.before)
                norm_apply(s, norm2, x3)

            def c_low(s):
                dve.wait_ge(hi3, s.n)
                nc.vector.tensor_tensor(flat(xt3_l), bank_c0[:, :], flat(xt3_h).bitcast(F32), ALU.subtract)\
                    .then_inc(lo3, 1)

            def c_top(s, b):
                dve.wait_ge(scored3, s.n * G - (G - 1 - b))
                nc.vector.tensor_copy(tick3[:, :], eps_c[:, 0:1])
                for h in range(H):
                    last = masked_max(z3[:, b, h, :], bank_c0[:, h * P:(h + 1) * P], top3[:, b, h:h + 1])
                last.then_inc(maxing3, 1)

            def c_neg(s, b):
                dve.wait_ge(maxing3, s.n * 6 - (5 - 3 * b))
                nc.vector.scalar_tensor_tensor(neg3[:, b, :], proj3[:, b, 0:H], -1.0, top3[:, b, :],
                                               ALU.mult, ALU.subtract).then_inc(maxing3, 1)

            def c_neg_max(s, b):
                dve.wait_ge(maxing3, s.n * 6 - (4 - 3 * b))
                nc.vector.scalar_tensor_tensor(neg_max3[:, b, :], neg3[:, b, :], SLOPE_L3, neg3[:, b, :],
                                               ALU.mult, ALU.min).then_inc(maxing3, 1)

            def c_biases(s, b):
                dve.wait_ge(maxing3, s.n * 6 - (3 - 3 * b))
                for k, factor in enumerate((1.0, SLOPE_L3)):
                    last = nc.vector.scalar_tensor_tensor(bias3[:, b, k, :], proj3[:, b, 0:H], factor,
                                                          neg_max3[:, b, :], ALU.mult, ALU.add)
                last.then_inc(biased3, 1)

            def c_weigh(s, b):
                dve.wait_ge(expd3, s.n * G - (G - 1 - b))
                for h in range(H):
                    last = nc.vector.scalar_tensor_tensor(p3[:, b, h, :], e3[:, b, 0, h, :], 1.0, e3[:, b, 1, h, :],
                                                          ALU.mult, ALU.max, accum_out=sum3[:, b, h:h + 1])
                last.then_inc(weighed3, 1)

            def c_invert(s, b):
                dve.wait_ge(weighed3, s.n * G - (G - 1 - b))
                nc.vector.reciprocal(rsum3[:, b, :], sum3[:, b, :]).then_inc(inverted3, 1)

            def c_elu_low(s, h):
                dve.wait_ge(elu_exp3, s.n * H - (H - 1 - h))
                nc.vector.tensor_scalar(elu3[:, h % 2, :], elu3[:, h % 2, :], 1.0, 1.0, ALU.min, ALU.subtract)\
                    .then_inc(elu_low3, 1)

            def c_elu(s, h):
                dve.wait_ge(elu_low3, s.n * H - (H - 1 - h))
                if s.again:
                    dve.wait_ge(h_lo, s.before * H - (H - 1 - h))
                nc.vector.tensor_tensor(h_s[:, h, :, :, :].rearrange("p c b n -> p (c b n)"),
                                        (bank_c0, bank_c1)[h % 2][:, :], elu3[:, h % 2, :], ALU.max)\
                    .then_inc(h_made, 1)

            def d_elu_low(s):
                dve.wait_ge(elu_exp4, s.n)
                nc.vector.tensor_scalar(elu4[:, :], elu4[:, :], 1.0, 1.0, ALU.min, ALU.subtract)\
                    .then_inc(elu_low4, 1)

            def d_elu(s):
                dve.wait_ge(elu_low4, s.n)
                if s.again:
                    dve.wait_ge(ff2_out, s.before)
                nc.vector.tensor_tensor(flat(o_s), bank_d0[:, :], elu4[:, :], ALU.max).then_inc(o_made, 1)

            def d_sum3(s):
                if not s.again:
                    dve.wait_ge(vec_in, 16 * VECTORS)
                dve.wait_ge(ff2_out, s.n)
                if s.again:
                    dve.wait_ge(norm3.done, s.before)
                nc.vector.tensor_tensor(norm3.y[:, :, :], bank_d1[:, :].rearrange("p (b f) -> p b f", b=G),
                                        fb2_bc[:, :].unsqueeze(1).to_broadcast([P, G, D]), ALU.add)\
                    .then_inc(norm3.summed, 1)

            def d_sum4(s):
                dve.wait_ge(x3_biased, s.n)
                if s.again:
                    dve.wait_ge(norm4.done, s.before)
                dve.wait_ge(scaled3, s.n)
                nc.vector.tensor_tensor(norm4.y[:, :, :], n3_g[:, :, :],
                                        x3_b[:, bass.ds(s.before % 2 * G, G), :], ALU.add)\
                    .then_inc(norm4.summed, 1)

            columns = [0]

            def attend(w, a_vec, dst):
                k = columns[0]
                if k >= 2:
                    dve.wait_ge(attended, k - 1)
                columns[0] += 1
                nc.vector.scalar_tensor_tensor(junk[:, k % 2, 0:w.shape[1]], w, 1.0, a_vec, ALU.mult, ALU.mult,
                                               accum_out=dst).then_inc(attended, 1)

            def attend_l1(s):
                if s.again:
                    return
                dve.wait_ge(a1_in, 16)
                dve.wait_ge(w1_in, 16)
                for c in range(DC):
                    for k in range(2):
                        attend(w1_s[:, c, 0:F1], a1_bc[:, k, :], w1_s[:, c, F1 + k:F1 + k + 1])
                dve.wait_ge(adj_t_in, 16)
                nc.vector.tensor_copy(adj_deg[:, 0, :], adj_ti[:, :]).then_inc(adj_made, 1)
                dve.wait_ge(made, 5)
                nc.vector.tensor_scalar(adj_deg[:, 1, :], ident[:, :], degree[:, 0:1], None, ALU.mult)\
                    .then_inc(adj_made, 1)

            def attend_heads(s):
                if s.again:
                    return
                dve.wait_ge(ah_in, 16)
                dve.wait_ge(wh_in, 16 * H)
                for h in range(H):
                    for c in range(DC):
                        for k in range(2):
                            attend(wh_s[:, c, h * D:(h + 1) * D], ah_bc[:, h, k, :],
                                   wha_s[:, c, k * H + h:k * H + h + 1])

            def attend_out(s, quarter):
                if s.again:
                    return
                dve.wait_ge(ao_in, 16)
                dve.wait_ge(wo_in, 16)
                for k in range(quarter * HC // 4, (quarter + 1) * HC // 4):
                    for j in range(2):
                        attend(wo_s[:, k, :], ao_bc[:, j, :], woa_s[:, k, j:j + 1])

            def degree_bias(s):
                if s.again:
                    return
                dve.wait_ge(b2_in, 16)
                nc.vector.tensor_scalar(deg_b[:, :], b2_bc, degree[:, 0:1], None, ALU.mult).then_inc(adj_made, 1)

            def turn(u):
                u.at(6, neg, att4)
                u.at(6, neg_max, att4)
                u.at(6, biases, att4)
                u.at(7, moments, norm4)
                u.at(5, c_biases, 1)
                u.at(4, b_conv_low, 1)
                u.at(3, a_norm)
                u.at(6, weigh, att4)
                u.at(2, weigh, att0)
                u.at(6, invert, att4)
                u.at(5, c_weigh, 1)
                u.at(2, invert, att0)
                u.at(5, c_invert, 1)
                u.at(4, b_conv_sum)
                u.at(4, statistics, norm2)
                u.at(4, moments, norm2)
                u.at(6, d_elu_low)
                u.at(6, d_elu)
                u.at(2, a_gate)
                u.at(4, b_norm2)
                u.at(3, attend_heads)
                u.at(3, top, att1)
                u.at(3, neg, att1)
                u.at(3, neg_max, att1)
                u.at(3, biases, att1)
                u.at(3, attend_out, 0)
                u.at(5, c_elu_low, 0)
                u.at(5, c_elu, 0)
                u.at(5, c_elu_low, 1)
                u.at(3, weigh, att1)
                u.at(5, c_elu, 1)
                u.at(2, degree_bias)
                u.at(2, a_sum)
                u.at(5, c_elu_low, 2)
                u.at(5, c_elu, 2)
                u.at(5, c_elu_low, 3)
                u.at(2, statistics, norm0)
                u.at(5, c_elu, 3)
                u.at(4, c_low)
                u.at(3, invert, att1)
                u.at(3, attend_out, 1)
                u.at(2, moments, norm0)
                u.at(6, d_sum3)
                u.at(6, statistics, norm3)
                u.at(3, b_sum)
                u.at(6, moments, norm3)
                u.at(4, c_top, 0)
                u.at(3, b_statistics)
                u.at(4, c_neg, 0)
                u.at(4, c_neg_max, 0)
                u.at(4, c_biases, 0)
                u.at(3, moments, norm1)
                u.at(3, attend_out, 2)
                u.at(1, attend_l1)
                u.at(1, top, att0)
                u.at(1, neg, att0)
                u.at(1, neg_max, att0)
                u.at(3, b_norm1)
                u.at(1, biases, att0)
                u.at(4, c_top, 1)
                u.at(4, c_weigh, 0)
                u.at(6, d_sum4)
                u.at(4, c_invert, 0)
                u.at(4, c_neg, 1)
                u.at(6, statistics, norm4)
                u.at(4, c_neg_max, 1)
                u.at(5, top, att4)
                u.at(3, attend_out, 3)
                u.at(3, b_conv_low, 0)

            dve.wait_ge(adj_in, 16)
            nc.vector.tensor_scalar(mask[:, :], adj_i[:, :], 0.0, FAR, ALU.is_equal, ALU.mult).then_inc(adj_made, 1)
            nc.vector.tensor_scalar(nonzero[:, :], adj_i[:, :], 0.0, None, ALU.not_equal).then_inc(adj_made, 1)
            nc.vector.reduce_sum(degree[:, :], adj_i[:, :], AX.X).then_inc(adj_made, 1)
            dve.wait_ge(adj_made, 2)
            nc.vector.reduce_max(has_neighbour[:, :], nonzero[:, :], AX.X).then_inc(adj_made, 1)
            dve.wait_ge(w0_in, 16)
            dve.wait_ge(a0_in, 32)
            for c in range(DC):
                for k in range(2):
                    attend(w0_s[:, c, 0:D], a0_bc[:, k, :], w0_s[:, c, D + k:D + k + 1])
            dve.wait_ge(weights_hi, 1)
            nc.vector.tensor_tensor(w0_l[:, :, :], w0_s[:, :, :], w0_h[:, :, :].bitcast(F32), ALU.subtract)\
                .then_inc(w0_lo, 1)
            dve.wait_ge(adj_made, 4)
            run_turns(dve, turn)


def kernel(x, adj, L0_gnn_W, L0_gnn_a_src, L0_gnn_a_dst, L1_gnn_W, L1_gnn_a, L2_gnn_W, L2_gnn_b,
           L3_gnn_W_heads, L3_gnn_a_heads, L3_gnn_W_out, L3_gnn_a_out, L3_gnn_w1, L3_gnn_b1,
           L3_gnn_w2, L3_gnn_b2, L3_gnn_ln_gamma, L3_gnn_ln_beta):
    import concourse.bacc as bacc
    from concourse.bass_utils import run_bass_kernel_spmd

    arrays = {
        "x_in": x, "x_t_in": np.asarray(x).transpose(0, 2, 1), "adj_in": adj, "adj_t_in": np.asarray(adj).T, "w0_in": L0_gnn_W,
        "a0_src_in": L0_gnn_a_src, "a0_dst_in": L0_gnn_a_dst, "w1_in": L1_gnn_W,
        "a1_in": np.asarray(L1_gnn_a).reshape(2, F1), "w2_t_in": np.asarray(L2_gnn_W).T, "b2_in": L2_gnn_b,
        "wh_in": L3_gnn_W_heads, "ah_in": L3_gnn_a_heads, "wo_in": L3_gnn_W_out, "ao_in": L3_gnn_a_out,
        "ff1_in": L3_gnn_w1, "fb1_t_in": np.asarray(L3_gnn_b1).reshape(DC, P).T, "ff2_in": L3_gnn_w2, "fb2_in": L3_gnn_b2,
        "gamma_in": L3_gnn_ln_gamma, "beta_in": L3_gnn_ln_beta,
    }
    arrays = {f"{k}_dram": np.ascontiguousarray(v) for k, v in arrays.items()}
    nc = bacc.Bacc("TRN2", target_bir_lowering=False, num_devices=1)
    args = [nc.dram_tensor(k, v.shape, mybir.dt.from_np(v.dtype), kind="ExternalInput").ap()
            for k, v in arrays.items()]
    out = nc.dram_tensor("out_dram", (B, N, D), F32, kind="ExternalOutput").ap()
    build(nc, *args, out)
    r = run_bass_kernel_spmd(nc, [arrays], core_ids=[0])
    return r.results[0]["out_dram"]
```
